# Optimizing a Trainium2 kernel written in Bass

```python
import numpy as np
import jax
import jax.numpy as jnp

def _softmax(x, axis=-1):
    return jax.nn.softmax(x, axis=axis)

def _gelu(x):
    return jax.nn.gelu(x, approximate=True)

def _silu(x):
    return jax.nn.silu(x)

def _sigmoid(x):
    return jax.nn.sigmoid(x)

def _layernorm(x, axis=-1, eps=1e-05):
    m = jnp.mean(x, axis=axis, keepdims=True)
    v = jnp.var(x, axis=axis, keepdims=True)
    return (x - m) / jnp.sqrt(v + eps)

def _scatter_add(tgt, idx, src, axis=0):
    return tgt.at[idx].add(src)

def _segment_sum(src, seg, n):
    return jax.ops.segment_sum(src, seg, n)
kernel_name = 'mk_prb_d2_jaxref_r8_e5b524'

def setup_inputs(seed: int=0):
    np.random.seed(seed)
    _w = jnp.asarray

    def _L0_attn_setup():
        import jax, jax.numpy as jnp
        import numpy as np
        N_HEADS, D_HEAD, D_EMBED = (16, 64, 128)
        BATCH, SEQ = (8, 128)
        WEIGHT_ALPHA = 1.0
        key = jax.random.key(seed)
        k1, k2, k3, k4, k5 = jax.random.split(key, 5)
        scale = WEIGHT_ALPHA / np.sqrt(D_EMBED)
        x = jax.random.normal(k1, (BATCH, SEQ, D_EMBED), dtype=jnp.float32)
        W_K = scale * jax.random.normal(k2, (N_HEADS, D_HEAD, D_EMBED), dtype=jnp.float32)
        W_Q = scale * jax.random.normal(k3, (N_HEADS, D_HEAD, D_EMBED), dtype=jnp.float32)
        W_V = scale * jax.random.normal(k4, (N_HEADS, D_HEAD, D_EMBED), dtype=jnp.float32)
        W_O = scale * jax.random.normal(k5, (D_EMBED, N_HEADS * D_HEAD), dtype=jnp.float32)
        return {'x': x, 'W_K': W_K, 'W_Q': W_Q, 'W_V': W_V, 'W_O': W_O}
    _L0_attn_in = _L0_attn_setup()

    def _L0_ffn_setup():
        import jax, jax.numpy as jnp
        import numpy as np
        EPS = 1e-05

        def _layernorm(x, w, b):
            mu = jnp.mean(x, axis=-1, keepdims=True)
            var = jnp.mean((x - mu) ** 2, axis=-1, keepdims=True)
            return (x - mu) * jax.lax.rsqrt(var + EPS) * w + b

        def _rope_tables(T, D, base=10000.0):
            inv_freq = 1.0 / base ** (jnp.arange(0, D, 2, dtype=jnp.float32) / D)
            t = jnp.arange(T, dtype=jnp.float32)
            freqs = jnp.einsum('i,j->ij', t, inv_freq)
            emb = jnp.concatenate([freqs, freqs], axis=-1)
            return (jnp.cos(emb), jnp.sin(emb))

        def _rotate_half(x):
            x1, x2 = (x[..., :x.shape[-1] // 2], x[..., x.shape[-1] // 2:])
            return jnp.concatenate([-x2, x1], axis=-1)

        def _attn(x, ln_w, ln_b, conv_w, attn_w, proj_w, n_head):
            B, T, C = x.shape
            D = C // n_head
            h = _layernorm(x, ln_w, ln_b)
            hc = jnp.transpose(h, (0, 2, 1))
            hc = jnp.pad(hc, ((0, 0), (0, 0), (2, 0)))
            hc = jax.lax.conv_general_dilated(hc, conv_w, window_strides=(1,), padding='VALID', dimension_numbers=('NCH', 'OIH', 'NCH'), feature_group_count=C)
            h = jnp.transpose(hc, (0, 2, 1))
            qkv = h @ attn_w
            q, k, v = jnp.split(qkv, 3, axis=-1)
            q = q.reshape(B, T, n_head, D)
            k = k.reshape(B, T, n_head, D)
            v = v.reshape(B, T, n_head, D)
            cos, sin = _rope_tables(T, D)
            cos = cos[None, :, None, :]
            sin = sin[None, :, None, :]
            q = q * cos + _rotate_half(q) * sin
            k = k * cos + _rotate_half(k) * sin
            scores = jnp.einsum('bqhd,bkhd->bhqk', q, k) / jnp.sqrt(jnp.float32(D))
            causal = jnp.tril(jnp.ones((T, T), dtype=bool))
            scores = jnp.where(causal, scores, jnp.float32(-1e+30))
            p = jax.nn.softmax(scores, axis=-1)
            y = jnp.einsum('bhqk,bkhd->bqhd', p, v).reshape(B, T, C)
            return y @ proj_w

        def _moe(x, ln_w, ln_b, router_w, expert_wv, expert_proj):
            h = _layernorm(x, ln_w, ln_b)
            logits = h @ router_w
            expert_idx = jnp.argmax(logits, axis=-1)
            E = router_w.shape[-1]
            out = jnp.zeros_like(x)
            for e in range(E):
                gv = h @ expert_wv[e]
                gate_raw, value = jnp.split(gv, 2, axis=-1)
                y = gate_raw * jax.nn.sigmoid(gate_raw) * value @ expert_proj[e]
                out = out + jnp.where((expert_idx == e)[..., None], y, 0.0)
            return out
        C, H, E, B, T = (128, 16, 4, 4, 128)
        Dff = 4 * C
        key = jax.random.key(seed)
        ks = jax.random.split(key, 8)
        s = 0.02
        return {'x': jax.random.normal(ks[0], (B, T, C), dtype=jnp.float32), 'ln1_w': jnp.ones((C,), jnp.float32), 'ln1_b': jnp.zeros((C,), jnp.float32), 'ln2_w': jnp.ones((C,), jnp.float32), 'ln2_b': jnp.zeros((C,), jnp.float32), 'conv_w': jax.random.normal(ks[1], (C, 1, 3), dtype=jnp.float32) * 0.1, 'attn_w': jax.random.normal(ks[2], (C, 3 * C), dtype=jnp.float32) * s, 'proj_w': jax.random.normal(ks[3], (C, C), dtype=jnp.float32) * s, 'router_w': jax.random.normal(ks[4], (C, E), dtype=jnp.float32) * s, 'expert_wv': jax.random.normal(ks[5], (E, C, 2 * Dff), dtype=jnp.float32) * s, 'expert_proj': jax.random.normal(ks[6], (E, Dff, C), dtype=jnp.float32) * s}
    _L0_ffn_in = _L0_ffn_setup()

    def _L1_attn_setup():
        import jax, jax.numpy as jnp
        import numpy as np
        N_EMBD = 128
        N_HEAD = 16
        HEAD_DIM = N_EMBD // N_HEAD
        BLOCK = 64
        SCALE = HEAD_DIM ** (-0.5)

        def _flash(q, k, v):
            BH, T, D = q.shape
            nb = T // BLOCK
            qb = q.reshape(BH, nb, BLOCK, D).transpose(1, 0, 2, 3)
            kb = k.reshape(BH, nb, BLOCK, D).transpose(1, 0, 2, 3)
            vb = v.reshape(BH, nb, BLOCK, D).transpose(1, 0, 2, 3)
            row = jnp.arange(BLOCK)

            def per_qblock(i, q_i):
                qpos = i * BLOCK + row[:, None]

                def step(carry, jkv):
                    m, l, o = carry
                    j, k_j, v_j = jkv
                    s = jnp.einsum('bqd,bkd->bqk', q_i, k_j) * SCALE
                    kpos = j * BLOCK + row[None, :]
                    s = jnp.where(kpos > qpos, -jnp.inf, s)
                    m_new = jnp.maximum(m, s.max(-1))
                    p = jnp.exp(s - m_new[..., None])
                    l_new = l * jnp.exp(m - m_new) + p.sum(-1)
                    ob = jnp.einsum('bqk,bkd->bqd', p, v_j)
                    o = o + (ob - o) * (l / l_new)[..., None]
                    return ((m_new, l_new, o), None)
                init = (jnp.full((BH, BLOCK), -jnp.inf, q.dtype), jnp.zeros((BH, BLOCK), q.dtype), jnp.zeros_like(q_i))
                (m, l, o), _ = jax.lax.scan(step, init, (jnp.arange(nb), kb, vb))
                return o / l[..., None]
            out = jax.vmap(per_qblock)(jnp.arange(nb), qb)
            return out.transpose(1, 0, 2, 3).reshape(BH, T, D)
        key = jax.random.key(seed)
        ks = jax.random.split(key, 4)
        x = jax.random.normal(ks[0], (4, 512, N_EMBD), jnp.float32)
        qkv_w = jax.random.normal(ks[1], (3 * N_EMBD, N_EMBD), jnp.float32) * 0.02
        qkv_b = jnp.zeros((3 * N_EMBD,), jnp.float32)
        proj_w = jax.random.normal(ks[2], (N_EMBD, N_EMBD), jnp.float32) * 0.02
        proj_b = jnp.zeros((N_EMBD,), jnp.float32)
        return {'x': x, 'qkv_w': qkv_w, 'qkv_b': qkv_b, 'proj_w': proj_w, 'proj_b': proj_b}
    _L1_attn_in = _L1_attn_setup()

    def _L1_ffn_setup():
        import jax, jax.numpy as jnp
        import numpy as np
        BLOCK = 16
        _GRID = jnp.array([0.0, 0.5, 1.0, 1.5, 2.0, 3.0, 4.0, 6.0], dtype=jnp.float32)
        _MID = jnp.array([0.25, 0.75, 1.25, 1.75, 2.5, 3.5, 5.0], dtype=jnp.float32)

        def fp4_quant_dequant(x):
            shape = x.shape
            xb = x.reshape(shape[:-1] + (shape[-1] // BLOCK, BLOCK))
            scale = jnp.max(jnp.abs(xb), axis=-1, keepdims=True) / 6.0
            scale = jnp.maximum(scale, jnp.float32(1e-12))
            xn = xb / scale
            idx = jnp.searchsorted(_MID, jnp.abs(xn))
            q = _GRID[idx] * jnp.sign(xn) * scale
            return q.reshape(shape)

        def fp4_linear(x, w):
            xq = fp4_quant_dequant(x)
            wq = fp4_quant_dequant(w)
            return jnp.einsum('bsk,nk->bsn', xq, wq)
        key = jax.random.key(seed)
        k1, k2, k3, k4 = jax.random.split(key, 4)
        H, I = (128, 352)
        x = jax.random.normal(k1, (4, 512, H), dtype=jnp.float32)
        w_gate = jax.random.normal(k2, (I, H), dtype=jnp.float32) * 0.02
        w_up = jax.random.normal(k3, (I, H), dtype=jnp.float32) * 0.02
        w_down = jax.random.normal(k4, (H, I), dtype=jnp.float32) * 0.02
        return {'x': x, 'w_gate': w_gate, 'w_up': w_up, 'w_down': w_down}
    _L1_ffn_in = _L1_ffn_setup()
    _d = {'L0_attn_x': _L0_attn_in['x'], 'L0_attn_W_K': _L0_attn_in['W_K'], 'L0_attn_W_Q': _L0_attn_in['W_Q'], 'L0_attn_W_V': _L0_attn_in['W_V'], 'L0_attn_W_O': _L0_attn_in['W_O'], 'L0_ffn_ln1_w': _L0_ffn_in['ln1_w'], 'L0_ffn_ln1_b': _L0_ffn_in['ln1_b'], 'L0_ffn_ln2_w': _L0_ffn_in['ln2_w'], 'L0_ffn_ln2_b': _L0_ffn_in['ln2_b'], 'L0_ffn_conv_w': _L0_ffn_in['conv_w'], 'L0_ffn_attn_w': _L0_ffn_in['attn_w'], 'L0_ffn_proj_w': _L0_ffn_in['proj_w'], 'L0_ffn_router_w': _L0_ffn_in['router_w'], 'L0_ffn_expert_wv': _L0_ffn_in['expert_wv'], 'L0_ffn_expert_proj': _L0_ffn_in['expert_proj'], 'L1_attn_qkv_w': _L1_attn_in['qkv_w'], 'L1_attn_qkv_b': _L1_attn_in['qkv_b'], 'L1_attn_proj_w': _L1_attn_in['proj_w'], 'L1_attn_proj_b': _L1_attn_in['proj_b'], 'L1_ffn_w_gate': _L1_ffn_in['w_gate'], 'L1_ffn_w_up': _L1_ffn_in['w_up'], 'L1_ffn_w_down': _L1_ffn_in['w_down']}
    _x0 = _d['L0_attn_x']
    _d['L0_attn_x'] = jax.random.normal(jax.random.fold_in(jax.random.key(seed), 1), (16, 512, 128), dtype=_x0.dtype)
    del _x0
    return _d

def reference(L0_attn_x, L0_attn_W_K, L0_attn_W_Q, L0_attn_W_V, L0_attn_W_O, L0_ffn_ln1_w, L0_ffn_ln1_b, L0_ffn_ln2_w, L0_ffn_ln2_b, L0_ffn_conv_w, L0_ffn_attn_w, L0_ffn_proj_w, L0_ffn_router_w, L0_ffn_expert_wv, L0_ffn_expert_proj, L1_attn_qkv_w, L1_attn_qkv_b, L1_attn_proj_w, L1_attn_proj_b, L1_ffn_w_gate, L1_ffn_w_up, L1_ffn_w_down):

    def _L0_attn_ref(x, W_K, W_Q, W_V, W_O):
        import jax, jax.numpy as jnp
        import numpy as np
        N_HEADS, D_HEAD, D_EMBED = (16, 64, 128)
        BATCH, SEQ = (8, 128)
        WEIGHT_ALPHA = 1.0
        b, seq, _ = x.shape
        d_head = W_K.shape[1]
        k = jnp.einsum('ahe,bce->bach', W_K, x)
        q = jnp.einsum('ahe,bce->bach', W_Q, x)
        v = jnp.einsum('ahe,bce->bach', W_V, x)
        scores = jnp.einsum('bach,baCh->bacC', k, q)
        mask = jnp.tril(jnp.ones((seq, seq), dtype=scores.dtype))
        masked = jnp.tril(scores) - 10000000000.0 * (1.0 - mask)
        attn = jax.nn.softmax(masked / np.sqrt(d_head), axis=-1)
        z = jnp.einsum('bach,bacC->baCh', v, attn)
        z_flat = z.transpose(0, 2, 1, 3).reshape(b, seq, -1)
        out = jnp.einsum('ef,bcf->bce', W_O, z_flat)
        return out

    def _L0_ffn_ref(x, ln1_w, ln1_b, ln2_w, ln2_b, conv_w, attn_w, proj_w, router_w, expert_wv, expert_proj):
        import jax, jax.numpy as jnp
        import numpy as np
        EPS = 1e-05

        def _layernorm(x, w, b):
            mu = jnp.mean(x, axis=-1, keepdims=True)
            var = jnp.mean((x - mu) ** 2, axis=-1, keepdims=True)
            return (x - mu) * jax.lax.rsqrt(var + EPS) * w + b

        def _rope_tables(T, D, base=10000.0):
            inv_freq = 1.0 / base ** (jnp.arange(0, D, 2, dtype=jnp.float32) / D)
            t = jnp.arange(T, dtype=jnp.float32)
            freqs = jnp.einsum('i,j->ij', t, inv_freq)
            emb = jnp.concatenate([freqs, freqs], axis=-1)
            return (jnp.cos(emb), jnp.sin(emb))

        def _rotate_half(x):
            x1, x2 = (x[..., :x.shape[-1] // 2], x[..., x.shape[-1] // 2:])
            return jnp.concatenate([-x2, x1], axis=-1)

        def _attn(x, ln_w, ln_b, conv_w, attn_w, proj_w, n_head):
            B, T, C = x.shape
            D = C // n_head
            h = _layernorm(x, ln_w, ln_b)
            hc = jnp.transpose(h, (0, 2, 1))
            hc = jnp.pad(hc, ((0, 0), (0, 0), (2, 0)))
            hc = jax.lax.conv_general_dilated(hc, conv_w, window_strides=(1,), padding='VALID', dimension_numbers=('NCH', 'OIH', 'NCH'), feature_group_count=C)
            h = jnp.transpose(hc, (0, 2, 1))
            qkv = h @ attn_w
            q, k, v = jnp.split(qkv, 3, axis=-1)
            q = q.reshape(B, T, n_head, D)
            k = k.reshape(B, T, n_head, D)
            v = v.reshape(B, T, n_head, D)
            cos, sin = _rope_tables(T, D)
            cos = cos[None, :, None, :]
            sin = sin[None, :, None, :]
            q = q * cos + _rotate_half(q) * sin
            k = k * cos + _rotate_half(k) * sin
            scores = jnp.einsum('bqhd,bkhd->bhqk', q, k) / jnp.sqrt(jnp.float32(D))
            causal = jnp.tril(jnp.ones((T, T), dtype=bool))
            scores = jnp.where(causal, scores, jnp.float32(-1e+30))
            p = jax.nn.softmax(scores, axis=-1)
            y = jnp.einsum('bhqk,bkhd->bqhd', p, v).reshape(B, T, C)
            return y @ proj_w

        def _moe(x, ln_w, ln_b, router_w, expert_wv, expert_proj):
            h = _layernorm(x, ln_w, ln_b)
            logits = h @ router_w
            expert_idx = jnp.argmax(logits, axis=-1)
            E = router_w.shape[-1]
            out = jnp.zeros_like(x)
            for e in range(E):
                gv = h @ expert_wv[e]
                gate_raw, value = jnp.split(gv, 2, axis=-1)
                y = gate_raw * jax.nn.sigmoid(gate_raw) * value @ expert_proj[e]
                out = out + jnp.where((expert_idx == e)[..., None], y, 0.0)
            return out
        n_head = 16
        x = x + _attn(x, ln1_w, ln1_b, conv_w, attn_w, proj_w, n_head)
        x = x + _moe(x, ln2_w, ln2_b, router_w, expert_wv, expert_proj)
        return x

    def _L1_attn_ref(x, qkv_w, qkv_b, proj_w, proj_b):
        import jax, jax.numpy as jnp
        import numpy as np
        N_EMBD = 128
        N_HEAD = 16
        HEAD_DIM = N_EMBD // N_HEAD
        BLOCK = 64
        SCALE = HEAD_DIM ** (-0.5)

        def _flash(q, k, v):
            BH, T, D = q.shape
            nb = T // BLOCK
            qb = q.reshape(BH, nb, BLOCK, D).transpose(1, 0, 2, 3)
            kb = k.reshape(BH, nb, BLOCK, D).transpose(1, 0, 2, 3)
            vb = v.reshape(BH, nb, BLOCK, D).transpose(1, 0, 2, 3)
            row = jnp.arange(BLOCK)

            def per_qblock(i, q_i):
                qpos = i * BLOCK + row[:, None]

                def step(carry, jkv):
                    m, l, o = carry
                    j, k_j, v_j = jkv
                    s = jnp.einsum('bqd,bkd->bqk', q_i, k_j) * SCALE
                    kpos = j * BLOCK + row[None, :]
                    s = jnp.where(kpos > qpos, -jnp.inf, s)
                    m_new = jnp.maximum(m, s.max(-1))
                    p = jnp.exp(s - m_new[..., None])
                    l_new = l * jnp.exp(m - m_new) + p.sum(-1)
                    ob = jnp.einsum('bqk,bkd->bqd', p, v_j)
                    o = o + (ob - o) * (l / l_new)[..., None]
                    return ((m_new, l_new, o), None)
                init = (jnp.full((BH, BLOCK), -jnp.inf, q.dtype), jnp.zeros((BH, BLOCK), q.dtype), jnp.zeros_like(q_i))
                (m, l, o), _ = jax.lax.scan(step, init, (jnp.arange(nb), kb, vb))
                return o / l[..., None]
            out = jax.vmap(per_qblock)(jnp.arange(nb), qb)
            return out.transpose(1, 0, 2, 3).reshape(BH, T, D)
        b, t, c = x.shape
        qkv = (x @ qkv_w.T + qkv_b).reshape(b, t, 3, N_HEAD, HEAD_DIM)
        q, k, v = (qkv[:, :, 0], qkv[:, :, 1], qkv[:, :, 2])

        def to_bh(a):
            return a.transpose(0, 2, 1, 3).reshape(b * N_HEAD, t, HEAD_DIM)
        o = _flash(to_bh(q), to_bh(k), to_bh(v))
        o = o.reshape(b, N_HEAD, t, HEAD_DIM).transpose(0, 2, 1, 3).reshape(b, t, c)
        return o @ proj_w.T + proj_b

    def _L1_ffn_ref(x, w_gate, w_up, w_down):
        import jax, jax.numpy as jnp
        import numpy as np
        BLOCK = 16
        _GRID = jnp.array([0.0, 0.5, 1.0, 1.5, 2.0, 3.0, 4.0, 6.0], dtype=jnp.float32)
        _MID = jnp.array([0.25, 0.75, 1.25, 1.75, 2.5, 3.5, 5.0], dtype=jnp.float32)

        def fp4_quant_dequant(x):
            shape = x.shape
            xb = x.reshape(shape[:-1] + (shape[-1] // BLOCK, BLOCK))
            scale = jnp.max(jnp.abs(xb), axis=-1, keepdims=True) / 6.0
            scale = jnp.maximum(scale, jnp.float32(1e-12))
            xn = xb / scale
            idx = jnp.searchsorted(_MID, jnp.abs(xn))
            q = _GRID[idx] * jnp.sign(xn) * scale
            return q.reshape(shape)

        def fp4_linear(x, w):
            xq = fp4_quant_dequant(x)
            wq = fp4_quant_dequant(w)
            return jnp.einsum('bsk,nk->bsn', xq, wq)
        gate = fp4_linear(x, w_gate)
        y = fp4_linear(x, w_up)
        h = jax.nn.silu(gate) * y
        return fp4_linear(h, w_down)
    x = L0_attn_x
    xn = _layernorm(x, axis=-1)
    x = x + _L0_attn_ref(xn, L0_attn_W_K, L0_attn_W_Q, L0_attn_W_V, L0_attn_W_O) + _L0_ffn_ref(xn, L0_ffn_ln1_w, L0_ffn_ln1_b, L0_ffn_ln2_w, L0_ffn_ln2_b, L0_ffn_conv_w, L0_ffn_attn_w, L0_ffn_proj_w, L0_ffn_router_w, L0_ffn_expert_wv, L0_ffn_expert_proj)
    xn = _layernorm(x, axis=-1)
    x = x + _L1_attn_ref(xn, L1_attn_qkv_w, L1_attn_qkv_b, L1_attn_proj_w, L1_attn_proj_b) + _L1_ffn_ref(xn, L1_ffn_w_gate, L1_ffn_w_up, L1_ffn_w_down)
    return x

_drawn_inputs = setup_inputs


def setup_inputs(seed=0):
    import zlib

    import numpy as np

    out = dict(_drawn_inputs(seed))
    spreads = {'L0_ffn_ln1_w': (1.0, 0.6),
     'L0_ffn_ln1_b': (0.0, 0.8),
     'L0_ffn_ln2_w': (1.0, 0.6),
     'L0_ffn_ln2_b': (0.0, 0.8),
     'L1_attn_qkv_b': (0.0, 2.0),
     'L1_attn_proj_b': (0.0, 2.0)}
    factors = {'L0_ffn_conv_w': 8.0,
     'L0_ffn_attn_w': 8.0,
     'L0_ffn_proj_w': 8.0,
     'L0_ffn_router_w': 8.0,
     'L0_ffn_expert_wv': 8.0,
     'L0_ffn_expert_proj': 8.0,
     'L1_attn_qkv_w': 41.31,
     'L1_attn_proj_w': 42.906,
     'L1_ffn_w_gate': 8.0,
     'L1_ffn_w_up': 8.0,
     'L1_ffn_w_down': 8.0}
    for name, (base, spread) in spreads.items():
        noise = np.random.default_rng([zlib.crc32(name.encode()), seed]).standard_normal(out[name].shape)
        drawn = base * np.exp(spread * noise) if base else spread * noise
        out[name] = jnp.asarray(drawn.astype(out[name].dtype))
    for name, factor in factors.items():
        out[name] = (out[name] * factor).astype(out[name].dtype)
    return out
```

```python
from contextlib import ExitStack

import numpy as np

import concourse.bass as bass
from concourse import mybir

ALU = mybir.AluOpType
ACT = mybir.ActivationFunctionType
AX = mybir.AxisListType
F32 = mybir.dt.float32
BF16 = mybir.dt.bfloat16
I32 = mybir.dt.int32

P = 128
C = 128
T = 512
NT = T // P
HEADS = 16
DA = 64
DB = C // HEADS
EXPERTS = 4
DFF = 512
CHUNKS = DFF // P
INNER = 352
INNER_PAD = 384
QBLOCK = 16
FLASH = 64
NFB = T // FLASH
PAIRS = HEADS // 2
EPS = 1e-5
FP4_MAX = 6.0
MASKED = -1e30
SCALE_B = float(DB) ** -0.5
PARTS = 3
SHIFT_ROW = 96
KS = PARTS * PARTS * DB
OFF = [sum(P * (u + 1) for u in range(t)) for t in range(NT)]
ROWLEN = sum(P * (u + 1) for u in range(NT))

HT_BANK = [0, 1, 5, 3]

K_ID = 0
K_UP = K_ID + P
K_LOW = K_UP + P
K_M1 = K_LOW + P
K_BLK = K_M1 + FLASH
K_COS = K_BLK + HEADS
K_SIN = K_COS + T
K_END = K_SIN + T


def shape_constants():
    k = np.zeros((P, K_END), np.float32)
    row, col = np.arange(P)[:, None], np.arange(P)[None, :]
    k[:, K_ID:K_ID + P] = row == col
    k[:, K_UP:K_UP + P] = np.where(col > row, np.float32(MASKED), 0)
    k[:, K_LOW:K_LOW + P] = np.where(row > col, np.float32(MASKED), 0)
    q, key = np.arange(P)[:, None] % FLASH, np.arange(FLASH)[None, :]
    k[:, K_M1:K_M1 + FLASH] = np.where(key > q, np.float32(MASKED), 0)
    k[:, K_BLK:K_BLK + HEADS] = np.arange(P)[:, None] // DB == np.arange(HEADS)[None, :]
    inv = (1.0 / 10000.0 ** (np.arange(0, DB, 2, dtype=np.float32) / np.float32(DB))).astype(np.float32)
    ang = np.arange(T, dtype=np.float32)[None, :] * inv[:, None]
    ang = np.concatenate([ang, ang], 0)
    sign = np.where(np.arange(DB) < DB // 2, -1.0, 1.0)[:, None]
    k[:, K_COS:K_COS + T] = np.repeat(np.cos(ang), HEADS, 0)
    k[:, K_SIN:K_SIN + T] = np.repeat(np.sin(ang) * sign, HEADS, 0)
    return k


PER = dict(
    x_loaded=16, xn_ready=4, xh_ready=4, xnT_psum=1, xhT_psum=1, xnT_ready=1, h_ready=1, conv_ready=1,
    qk_psum=4, bv_psum=1, bv_ready=1, split_ready=6, stack_loaded=16 * 18, bs_psum=16, bmax_ready=16,
    mxT_psum=1, mx_split=3, shift_loaded=48, bst_psum=32, bexp_done=32, bav_done=16, by_ready=4,
    byT_psum=4, yn_ready=4, ynT_psum=1, ynT_ready=1, bo_psum=1, xh2_ready=4, xh2T_psum=1, h2T_ready=1,
    logits_psum=1, gv_psum=16, silu_done=16, moe_y=16, down_psum=4, moe_acc=4,
    avp_psum=8, av_ready=8, g_psum=16, g_ready=16, as_psum=64, amax=64, aexp_done=64, vn_ready=16,
    zav_done=8, z_ready=8, ao_psum=1, xn2_ready=4, xq_ready=1, xn2T_psum=1, xn2T_ready=1,
    kqv1_psum=3, kq1_ready=2, qbd_ready=1, s1_psum=1, sub1_ready=1, dm1_ready=1, fac1_ready=1, p1_ready=1,
    pw1_ready=1, pT1_psum=8, pT1_act=4, pT1_dve=4, o1_psum=1, oT1_ready=1, pr1_psum=1,
    xqT_psum=1, xqT_ready=1, gu_psum=4, sgf_done=4, hf_done=4, hq_ready=1, hqT_psum=4, hqT_ready=4,
    dn_psum=1, out_ready=1, out_stored=16,
)
DVE_STEPS = 237
PREP_LOADS = 27


def build_layers(nc, w, x, consts, out):
    B = x.shape[0]
    with ExitStack() as ctx:
        def sb(name, shape, dt=F32):
            return ctx.enter_context(nc.sbuf_tensor(name, shape, dt))

        def sem(name):
            return ctx.enter_context(nc.semaphore(name))

        def view(buf, shape, at=0, dt=F32):
            n = int(np.prod(shape[1:])) * (2 if dt == BF16 else 4) // 4
            a = buf[0:shape[0], at:at + n]
            if dt != F32:
                a = a.bitcast(dt)
            if len(shape) == 2:
                return a
            names = "abcd"[:len(shape) - 1]
            return a.rearrange(f"p ({' '.join(names)}) -> p {' '.join(names)}",
                               **dict(zip(names[1:], shape[2:])))

        NQ = NT * INNER // QBLOCK
        share_a = sb("share_a", [P, 4096])
        share_b = sb("share_b", [P, 4 * NQ * QBLOCK])
        share_c = sb("share_c", [P, 4096])
        share_f = sb("share_f", [P, 1024])
        share_g = sb("share_g", [P, 1024])
        share_h = sb("share_h", [P, 1024])
        share_i = sb("share_i", [P, 4096])
        share_j = sb("share_j", [P, T])

        kc = sb("kc", [P, K_END])
        ident = kc[:, K_ID:K_ID + P]
        ident_b = sb("ident_b", [P, P], BF16)
        up_b = sb("up_b", [P, P], BF16)
        low_b = sb("low_b", [P, P], BF16)
        m1_b = sb("m1_b", [P, FLASH], BF16)
        blk = kc[:, K_BLK:K_BLK + HEADS]
        cosT, sinT = kc[:, K_COS:K_COS + T], kc[:, K_SIN:K_SIN + T]
        wkq = view(share_a, [DA, 2, HEADS, C])
        raw = view(share_i, [P, 8, C])
        raw2 = view(share_i, [P, 8 * C], 1024)
        mg = sb("mg", [P, HEADS, C])
        wvT = sb("wvT", [C, HEADS * DA])
        woT = sb("woT", [P, PAIRS, C])
        ln1 = sb("ln1", [C, 4])
        convw = sb("convw", [C, 3])
        wqkv = sb("wqkv", [C, 3 * C])
        wrot = sb("wrot", [C, 4, DB, HEADS])
        wproj = sb("wproj", [C, C])
        wrt = sb("wrt", [C, EXPERTS])
        wgv = sb("wgv", [C, EXPERTS, 2 * DFF])
        wdn = sb("wdn", [P, EXPERTS, CHUNKS, C])
        w1raw = view(share_c, [P, 4, C], 2048)
        w1T = sb("w1T", [C, 4, C])
        b1col = sb("b1col", [P, 2])
        brow = sb("brow", [1, 2 * C])
        ones = sb("ones", [1, P])
        b1bc = sb("b1bc", [P, 2, C])
        wguR = view(share_c, [P, 6, C])
        wdR = view(share_c, [P, INNER_PAD], 1024)
        wguT = sb("wguT", [C, 2, INNER_PAD])
        wdT = sb("wdT", [P, 3, C])

        xin = sb("xin", [P, NT, C])
        xn = sb("xn", [P, NT, C])
        xh = sb("xh", [P, NT, C])
        xnT = sb("xnT", [C, T])
        hpad = sb("hpad", [C, T + 2])
        hc = view(share_j, [C, T])
        rope = view(share_f, [P, 2, T])
        part = view(share_c, [P, 2, PARTS, T], 0, BF16)
        kst = sb("kst", [P, HEADS, T], BF16)
        qst = sb("qst", [P, HEADS, T], BF16)
        vaug = sb("vaug", [P, NT, HEADS, 32])
        nmx = sb("nmx", [P, 2 * HEADS, NT])
        mx3 = sb("mx3", [HEADS * NT, PARTS, P], BF16)
        mxr = sb("mxr", [HEADS * NT, P])
        pt = view(share_i, [P, 2, 4, T])
        ys = view(share_b, [P, 4, T])
        rb = sb("rb", [P, NT, HEADS])
        yn = view(share_f, [P, NT, C])
        ynT = view(share_j, [C, T])
        x1 = sb("x1", [P, NT, C])
        h2T = view(share_g, [C, T])
        lg = sb("lg", [P, NT, EXPERTS])
        lmax = sb("lmax", [P, NT])
        hot = sb("hot", [P, NT, EXPERTS])
        taken = sb("taken", [P, NT])
        sg = view(share_h, [P, 2, T])
        ym = view(share_a, [P, 2, CHUNKS, T])
        va = view(share_a, [P, NT, HEADS * DA])
        gs = view(share_g, [P, 2, T])
        nma = sb("nma", [P, HEADS, NT])
        la = sb("la", [P, HEADS, NT])
        rla = sb("rla", [P, HEADS, NT])
        pa = view(share_b, [P, 4, ROWLEN])
        vn = view(share_h, [P, 4, NT, DA])
        zT = view(share_c, [P, PAIRS, T])
        xp = sb("xp", [P, NT, C])
        k1T = view(share_g, [C, T])
        q1T = sb("q1T", [C, FLASH])
        v1 = view(share_g, [P, NT, C], T)
        qbd = view(share_a, [C, HEADS, FLASH])
        ss = view(share_c, [P, PAIRS, NFB, FLASH])
        bm = sb("bm", [P, PAIRS, NFB])
        rm = sb("rm", [P, PAIRS, NFB])
        dm = sb("dm", [P, PAIRS, NFB])
        ll = sb("ll", [P, PAIRS, NFB])
        rl = sb("rl", [P, PAIRS, NFB])
        rr = sb("rr", [P, PAIRS, NFB])
        co = sb("co", [P, PAIRS, NFB])
        cc = sb("cc", [P, PAIRS])
        om = view(share_a, [C, HEADS, FLASH], 1024)
        oT = sb("oT", [C, FLASH])
        xq = view(share_f, [P, NT, C])
        xqT = view(share_f, [C, T], T)
        sgf = view(share_h, [P, 2, INNER])
        hf = view(share_i, [P, NT, INNER])
        hq = view(share_a, [P, NT, INNER_PAD], 2048)
        hqT = view(share_i, [P, NT, 3, P], 2048)
        yout = xh
        st = sb("st", [P, NT, 6])
        mv = sb("mv", [P, 3, NT])
        ve = sb("ve", [P, NT])
        ri = sb("ri", [P, NT], I32)
        ry = sb("ry", [P, NT])
        rt = sb("rt", [P, NT])
        qa = view(share_b, [P, NQ, QBLOCK], 0 * NQ * QBLOCK)
        qc = view(share_b, [P, NQ, QBLOCK], 1 * NQ * QBLOCK)
        qd = view(share_b, [P, NQ, QBLOCK], 2 * NQ * QBLOCK)
        qe = view(share_b, [P, NQ, QBLOCK], 3 * NQ * QBLOCK)
        qm = sb("qm", [P, NQ])
        qr = sb("qr", [P, NQ])

        ps = ctx.enter_context(nc.psum_tensor("ps", [P, 8, 512], F32))

        x_loaded = sem("x_loaded")
        xn_ready = sem("xn_ready")
        xh_ready = sem("xh_ready")
        xnT_psum = sem("xnT_psum")
        xhT_psum = sem("xhT_psum")
        xnT_ready = sem("xnT_ready")
        h_ready = sem("h_ready")
        conv_ready = sem("conv_ready")
        qk_psum = sem("qk_psum")
        bv_psum = sem("bv_psum")
        bv_ready = sem("bv_ready")
        split_ready = sem("split_ready")
        stack_loaded = sem("stack_loaded")
        bs_psum = sem("bs_psum")
        bmax_ready = sem("bmax_ready")
        mxT_psum = sem("mxT_psum")
        mx_split = sem("mx_split")
        shift_loaded = sem("shift_loaded")
        bst_psum = sem("bst_psum")
        bexp_done = sem("bexp_done")
        bav_done = sem("bav_done")
        by_ready = sem("by_ready")
        byT_psum = sem("byT_psum")
        yn_ready = sem("yn_ready")
        ynT_psum = sem("ynT_psum")
        ynT_ready = sem("ynT_ready")
        bo_psum = sem("bo_psum")
        xh2_ready = sem("xh2_ready")
        xh2T_psum = sem("xh2T_psum")
        h2T_ready = sem("h2T_ready")
        logits_psum = sem("logits_psum")
        gv_psum = sem("gv_psum")
        silu_done = sem("silu_done")
        moe_y = sem("moe_y")
        down_psum = sem("down_psum")
        moe_acc = sem("moe_acc")
        avp_psum = sem("avp_psum")
        av_ready = sem("av_ready")
        g_psum = sem("g_psum")
        g_ready = sem("g_ready")
        as_psum = sem("as_psum")
        amax = sem("amax")
        aexp_done = sem("aexp_done")
        vn_ready = sem("vn_ready")
        zav_done = sem("zav_done")
        z_ready = sem("z_ready")
        ao_psum = sem("ao_psum")
        xn2_ready = sem("xn2_ready")
        xq_ready = sem("xq_ready")
        xn2T_psum = sem("xn2T_psum")
        xn2T_ready = sem("xn2T_ready")
        kqv1_psum = sem("kqv1_psum")
        kq1_ready = sem("kq1_ready")
        qbd_ready = sem("qbd_ready")
        s1_psum = sem("s1_psum")
        sub1_ready = sem("sub1_ready")
        dm1_ready = sem("dm1_ready")
        fac1_ready = sem("fac1_ready")
        p1_ready = sem("p1_ready")
        pw1_ready = sem("pw1_ready")
        pT1_psum = sem("pT1_psum")
        pT1_act = sem("pT1_act")
        pT1_dve = sem("pT1_dve")
        o1_psum = sem("o1_psum")
        oT1_ready = sem("oT1_ready")
        pr1_psum = sem("pr1_psum")
        xqT_psum = sem("xqT_psum")
        xqT_ready = sem("xqT_ready")
        gu_psum = sem("gu_psum")
        sgf_done = sem("sgf_done")
        hf_done = sem("hf_done")
        hq_ready = sem("hq_ready")
        hqT_psum = sem("hqT_psum")
        hqT_ready = sem("hqT_ready")
        dn_psum = sem("dn_psum")
        out_ready = sem("out_ready")
        out_stored = sem("out_stored")
        weights_loaded = sem("weights_loaded")
        prep_pe = sem("prep_pe")
        prep_act = sem("prep_act")
        prep_dve = sem("prep_dve")
        dve_step = sem("dve_step")

        block = ctx.enter_context(nc.Block())

        PREP_DVE = 52
        PREP_PE = 15
        PREP_ACT = 11

        def prep_over(eng):
            eng.wait_ge(prep_dve, PREP_DVE)
            eng.wait_ge(prep_act, PREP_ACT)

        @block.sync
        def _(sp):
            col = lambda a: a.rearrange("(p a) -> p a", a=1)
            loads = [
                (kc[:, :], consts),
                (wkq[:, 0], w["L0_attn_W_K"].rearrange("a h e -> h a e")),
                (wkq[:, 1], w["L0_attn_W_Q"].rearrange("a h e -> h a e")),
                (raw[:, :, :], w["L0_attn_W_V"].rearrange("(n a) h e -> (a h) n e", a=2)),
                (raw2[:, :], w["L0_attn_W_O"]),
                (ln1[:, 0:1], col(w["L0_ffn_ln1_w"])), (ln1[:, 1:2], col(w["L0_ffn_ln1_b"])),
                (ln1[:, 2:3], col(w["L0_ffn_ln2_w"])), (ln1[:, 3:4], col(w["L0_ffn_ln2_b"])),
                (convw[:, :], w["L0_ffn_conv_w"].rearrange("c a k -> c (a k)")),
                (wqkv[:, :], w["L0_ffn_attn_w"]),
                (wproj[:, :], w["L0_ffn_proj_w"]),
                (wrt[:, :], w["L0_ffn_router_w"]),
                (wgv[:, :, :], w["L0_ffn_expert_wv"].rearrange("e c f -> c e f")),
                (wdn[:, :, :, :], w["L0_ffn_expert_proj"].rearrange("e (k p) c -> p e k c", p=P)),
                (w1raw[:, 0:3, :], w["L1_attn_qkv_w"].rearrange("(n p) c -> p n c", p=P)),
                (w1raw[:, 3, :], w["L1_attn_proj_w"]),
                (b1col[:, 0:1], col(w["L1_attn_qkv_b"][0:C])),
                (b1col[:, 1:2], col(w["L1_attn_qkv_b"][C:2 * C])),
                (brow[:, 0:C], w["L1_attn_qkv_b"][2 * C:3 * C].rearrange("(a c) -> a c", a=1)),
                (brow[:, C:2 * C], w["L1_attn_proj_b"].rearrange("(a c) -> a c", a=1)),
            ]
            for dst, src in loads:
                sp.dma_start(dst, src).then_inc(weights_loaded, 16)
            sp.wait_ge(prep_dve, 4)
            for n, name in enumerate(("L1_ffn_w_gate", "L1_ffn_w_up")):
                sp.dma_start(wguR[:, 3 * n:3 * n + 2, :],
                             w[name][0:2 * P, :].rearrange("(n p) c -> p n c", p=P)).then_inc(weights_loaded, 16)
                sp.dma_start(wguR[0:INNER - 2 * P, 3 * n + 2, :],
                             w[name][2 * P:INNER, :]).then_inc(weights_loaded, 16)
            sp.dma_start(wdR[:, 0:INNER], w["L1_ffn_w_down"]).then_inc(weights_loaded, 16)
            sp.dma_start(vaug[0:1, 0, 0, 0:1], consts[0:1, 0:1]).then_inc(weights_loaded, 16)
            assert len(loads) + 6 == PREP_LOADS
            prep_over(sp)

            with sp.Fori(0, B) as i:
                for z, stack in ((0, qst), (1, kst)):
                    for a in range(PARTS):
                        sp.wait_ge(split_ready, i * PER["split_ready"] + 3 * z + a + 1)
                        for b in range(PARTS):
                            r = DB * (PARTS * a + b) if z == 0 else DB * (PARTS * b + a)
                            sp.dma_start(stack[r:r + DB, :, :], part[:, z, a, :]
                                         ).then_inc(stack_loaded, 16)
                for a in range(PARTS):
                    sp.wait_ge(mx_split, i * PER["mx_split"] + a + 1)
                    sp.dma_start(qst[SHIFT_ROW + a:SHIFT_ROW + a + 1, :, :].rearrange(
                        "o h (t q) -> o (h t) q", t=NT), mx3[:, a, :]).then_inc(shift_loaded, 16)

        @block.scalar
        def _(act):
            def evac(n, dst, src, scale=1.0):
                act.wait_ge(prep_pe, n)
                nc.scalar.activation(dst, src, ACT.Copy, scale=scale).then_inc(prep_act, 1)

            for g in range(4):
                evac(g + 1, mg[:, 4 * g:4 * g + 4, :].rearrange("p h c -> p (h c)"), ps[:, g, :], DA ** -0.5)
            for g in range(2):
                evac(5 + g, wvT[:, 512 * g:512 * g + 512], ps[:, 4 + g, :])
            for g in range(2):
                evac(7 + g, woT[:, 4 * g:4 * g + 4, :].rearrange("p h c -> p (h c)"), ps[:, 6 + g, :])
            evac(9, w1T[:, :, :].rearrange("p h c -> p (h c)"), ps[:, 0, :])
            evac(10, b1bc[:, :, :].rearrange("p h c -> p (h c)"), ps[:, 1, 0:2 * C])
            evac(15, wguT[:, :, :].rearrange("p a c -> p (a c)"), ps[:, 2:4, 0:INNER_PAD])
            prep_over(act)

            with act.Fori(0, B) as i:
                copy = nc.scalar.copy
                act.dma_start(xin[:, :, :],
                              x[bass.ds(i, 1), :, :].rearrange("a (t p) c -> p (a t) c", p=P)
                              ).then_inc(x_loaded, 16)
                act.wait_ge(xnT_psum, i * PER["xnT_psum"] + 1)
                copy(xnT[:, :], ps[:, 0, :]).then_inc(xnT_ready, 1)
                act.wait_ge(xhT_psum, i * PER["xhT_psum"] + 1)
                nc.scalar.activation(hpad[:, 2:T + 2], ps[:, 1, :], ACT.Identity, bias=ln1[:, 1:2],
                                          scale=ln1[:, 0:1]).then_inc(h_ready, 1)
                act.wait_ge(bv_psum, i * PER["bv_psum"] + 1)
                copy(vaug[:, :, :, 0:DB].rearrange("p t h d -> p (t h) d"),
                          ps[:, 6, :].rearrange("p (n d) -> p n d", d=DB)).then_inc(bv_ready, 1)

                def b_exp(n):
                    j = n % NT
                    if n >= 2:
                        act.wait_ge(bav_done, i * PER["bav_done"] + n - 1)
                    for half in range(2):
                        m = 2 * n + half
                        act.wait_ge(bst_psum, i * PER["bst_psum"] + m + 1)
                        b = 2 * (m % 3)
                        nc.scalar.activation(pt[:, n % 2, 2 * half:2 * half + 2, 0:T - j * P],
                                                  ps[:, b:b + 2, 0:T - j * P], ACT.Exp, scale=SCALE_B)\
                                                     .then_inc(bexp_done, 1)

                def b_evac(g):
                    act.wait_ge(bav_done, i * PER["bav_done"] + 4 * g + 4)
                    copy(ys[:, g, :], ps[:, 6 + g % 2, :]).then_inc(by_ready, 1)

                for n in range(16):
                    b_exp(n)
                    if n >= 4 and n % 4 == 0:
                        b_evac(n // 4 - 1)
                b_evac(3)
                act.wait_ge(ynT_psum, i * PER["ynT_psum"] + 1)
                copy(ynT[:, :], ps[:, 4, :]).then_inc(ynT_ready, 1)
                act.wait_ge(xh2T_psum, i * PER["xh2T_psum"] + 1)
                nc.scalar.activation(h2T[:, :], ps[:, 6, :], ACT.Identity, bias=ln1[:, 3:4],
                                          scale=ln1[:, 2:3]).then_inc(h2T_ready, 1)
                for n in range(16):
                    act.wait_ge(gv_psum, i * PER["gv_psum"] + n + 1)
                    if n >= 2:
                        act.wait_ge(moe_y, i * PER["moe_y"] + n - 1)
                    nc.scalar.activation(sg[:, n % 2, :], ps[:, 2 * (n % 3), :], ACT.Silu).then_inc(silu_done, 1)

                for n in range(8):
                    act.wait_ge(avp_psum, i * PER["avp_psum"] + n + 1)
                    copy(va[:, n // 2, 512 * (n % 2):512 * (n % 2) + 512], ps[:, n % 4, :]).then_inc(av_ready, 1)

                def g_evac(h):
                    act.wait_ge(g_psum, i * PER["g_psum"] + h + 1)
                    if h >= 2:
                        act.wait_ge(as_psum, i * PER["as_psum"] + 4 * (h - 1))
                    copy(gs[:, h % 2, :], ps[:, 4 + h % 2, :]).then_inc(g_ready, 1)

                def z_evac(p):
                    act.wait_ge(zav_done, i * PER["zav_done"] + p + 1)
                    copy(zT[:, p, :], ps[:, 6 + p % 2, :]).then_inc(z_ready, 1)

                g_evac(0)
                for h in range(HEADS):
                    if h + 1 < HEADS:
                        g_evac(h + 1)
                    if h >= 4:
                        act.wait_ge(zav_done, i * PER["zav_done"] + (h - 4) // 2 + 1)
                    for t in range(NT):
                        act.wait_ge(amax, i * PER["amax"] + 4 * h + t + 1)
                        nc.scalar.activation(pa[:, h % 4, OFF[t]:OFF[t] + P * (t + 1)],
                                                  ps[:, t, 0:P * (t + 1)], ACT.Exp, bias=nma[:, h, t:t + 1],
                                                  accum_out=la[:, h, t:t + 1]).then_inc(aexp_done, 1)
                    if h % 2 and h >= 3:
                        z_evac((h - 3) // 2)
                z_evac(PAIRS - 1)

                act.wait_ge(xn2T_psum, i * PER["xn2T_psum"] + 1)
                copy(xnT[:, :], ps[:, 0, :]).then_inc(xn2T_ready, 1)
                act.wait_ge(kqv1_psum, i * PER["kqv1_psum"] + 1)
                nc.scalar.activation(k1T[:, :], ps[:, 1, :], ACT.Identity, bias=b1col[:, 1:2]).then_inc(kq1_ready, 1)
                act.wait_ge(kqv1_psum, i * PER["kqv1_psum"] + 2)
                nc.scalar.activation(q1T[:, :], ps[:, 2, 0:FLASH], ACT.Identity, bias=b1col[:, 0:1])\
                   .then_inc(kq1_ready, 1)
                act.wait_ge(sub1_ready, i * PER["sub1_ready"] + 1)
                nc.scalar.activation(ss[:, :, :, :], ss[:, :, :, :], ACT.Exp, scale=SCALE_B).then_inc(p1_ready, 1)
                act.wait_ge(dm1_ready, i * PER["dm1_ready"] + 1)
                nc.scalar.activation(dm[:, :, 1:NFB], dm[:, :, 1:NFB], ACT.Exp, scale=SCALE_B).then_inc(fac1_ready, 1)
                pT = share_i
                for n in range(0, 8, 2):
                    act.wait_ge(pT1_psum, i * PER["pT1_psum"] + n + 1)
                    copy(pT[:, 512 * n:512 * n + 512], ps[:, n, :]).then_inc(pT1_act, 1)
                act.wait_ge(xqT_psum, i * PER["xqT_psum"] + 1)
                copy(xqT[:, :], ps[:, 3, :]).then_inc(xqT_ready, 1)
                for t in range(NT):
                    act.wait_ge(gu_psum, i * PER["gu_psum"] + t + 1)
                    if t >= 2:
                        act.wait_ge(hf_done, i * PER["hf_done"] + t - 1)
                    nc.scalar.activation(sgf[:, t % 2, :], ps[:, 4 + 2 * (t % 2), 0:INNER], ACT.Silu)\
                       .then_inc(sgf_done, 1)
                for t in range(NT):
                    act.wait_ge(hqT_psum, i * PER["hqT_psum"] + t + 1)
                    copy(hqT[:, t, :, :].rearrange("p a b -> p (a b)"), ps[:, HT_BANK[t], 0:3 * P])\
                       .then_inc(hqT_ready, 1)
                act.wait_ge(out_ready, i * PER["out_ready"] + 1)
                act.dma_start(out[bass.ds(i, 1), :, :].rearrange("a (t p) c -> p (a t) c", p=P),
                              yout[:, :, :]).then_inc(out_stored, 16)
                act.wait_ge(out_stored, i * PER["out_stored"] + 16)

        @block.vector
        def _(dve):
            v = nc.vector

            def layer_norm(src, dst, link, finish):
                for t in range(NT):
                    link(v.bn_stats(st[:, t, :], src[:, t, :]), t == NT - 1)
                link(v.tensor_tensor(mv[:, 0, :], st[:, :, 1], st[:, :, 4], ALU.add), False)
                link(v.tensor_tensor(mv[:, 1, :], st[:, :, 1], st[:, :, 4], ALU.subtract), False)
                link(v.tensor_tensor(mv[:, 2, :], st[:, :, 2], st[:, :, 5], ALU.add))
                link(v.tensor_scalar(mv[:, 0, :], mv[:, 0, :], 0.5, None, ALU.mult), False)
                link(v.scalar_tensor_tensor(out=mv[:, 1, :], in0=mv[:, 1, :], scalar=0.25, in1=mv[:, 1, :],
                                            op0=ALU.mult, op1=ALU.mult))
                link(v.scalar_tensor_tensor(out=ve[:, :], in0=mv[:, 2, :], scalar=1.0 / C, in1=mv[:, 1, :],
                                            op0=ALU.mult, op1=ALU.add))
                link(v.tensor_scalar(ve[:, :], ve[:, :], EPS, None, ALU.add))
                link(v.tensor_scalar(ri[:, :], ve[:, :].bitcast(I32), 1, None, ALU.logical_shift_right))
                link(v.tensor_scalar(ry[:, :].bitcast(I32), ri[:, :], -1.0, float(0x5f3759df), ALU.mult, ALU.add))
                for _ in range(4):
                    link(v.scalar_tensor_tensor(out=rt[:, :], in0=ry[:, :], scalar=-0.5, in1=ry[:, :],
                                                op0=ALU.mult, op1=ALU.mult))
                    link(v.tensor_tensor(rt[:, :], rt[:, :], ve[:, :], ALU.mult))
                    link(v.scalar_tensor_tensor(out=ry[:, :], in0=rt[:, :], scalar=1.5, in1=ry[:, :],
                                                op0=ALU.add, op1=ALU.mult))
                for t in range(NT):
                    finish(v.tensor_scalar(dst[:, t, :], src[:, t, :], mv[:, 0, t:t + 1], ry[:, t:t + 1],
                                           ALU.subtract, ALU.mult))

            def fp4(src, dst, n, link, finish):
                blocks = lambda a: a[:, 0:n, :]
                a, s, u, x2 = blocks(qa), blocks(qc), blocks(qd), blocks(qe)
                m, r = qm[:, 0:n], qr[:, 0:n]
                over = lambda z: z.unsqueeze(2).to_broadcast([P, n, QBLOCK])
                link(v.scalar_tensor_tensor(out=a, in0=src, scalar=-1.0, in1=src, op0=ALU.mult, op1=ALU.max))
                link(v.tensor_reduce(m, a, AX.X, ALU.max))
                link(v.tensor_scalar(m, m, 1.0 / FP4_MAX, 1e-12, ALU.mult, ALU.max))
                link(v.reciprocal(r, m))
                link(v.tensor_tensor(a, a, over(r), ALU.mult))
                link(v.tensor_scalar(s, a, 0.25, None, ALU.is_gt), False)
                link(v.tensor_scalar(u, a, 2.5, None, ALU.is_gt), False)
                link(v.tensor_scalar(x2, a, 5.0, 2.0, ALU.is_gt, ALU.mult))
                link(v.scalar_tensor_tensor(out=u, in0=a, scalar=3.5, in1=u, op0=ALU.is_gt, op1=ALU.add), False)
                link(v.scalar_tensor_tensor(out=s, in0=a, scalar=0.75, in1=s, op0=ALU.is_gt, op1=ALU.add))
                link(v.tensor_tensor(u, u, x2, ALU.add), False)
                link(v.scalar_tensor_tensor(out=s, in0=a, scalar=1.25, in1=s, op0=ALU.is_gt, op1=ALU.add))
                link(v.scalar_tensor_tensor(out=s, in0=a, scalar=1.75, in1=s, op0=ALU.is_gt, op1=ALU.add))
                link(v.scalar_tensor_tensor(out=s, in0=u, scalar=2.0, in1=s, op0=ALU.mult, op1=ALU.add))
                link(v.scalar_tensor_tensor(out=u, in0=s, scalar=0.5, in1=over(m), op0=ALU.mult, op1=ALU.mult))
                finish(v.scalar_tensor_tensor(out=dst.bitcast(I32), in0=src.bitcast(I32), scalar=-2 ** 31,
                                              in1=u.bitcast(I32), op0=ALU.bitwise_and, op1=ALU.bitwise_or))

            count = [0]

            def link0(ins, settle=True):
                count[0] += 1
                ins.then_inc(prep_dve, 1)
                if settle:
                    dve.wait_ge(prep_dve, count[0])

            link0(v.memset(wguR[:, :, :], 0.0), False)
            link0(v.memset(wdR[:, :], 0.0), False)
            link0(v.memset(vaug[:, :, :, :], 1.0), False)
            link0(v.memset(hpad[:, 0:2], 0.0), False)
            link0(v.memset(ones[:, :], 1.0), False)
            link0(v.memset(nmx[:, :, :], 0.0), False)
            link0(v.memset(kst[:, :, :].bitcast(I32), 0), False)
            link0(v.memset(qst[:, :, :].bitcast(I32), 0))
            link0(v.memset(kst[SHIFT_ROW:P, :, :], 1.0))
            dve.wait_ge(weights_loaded, 16 * PREP_LOADS)
            link0(v.tensor_copy(ident_b[:, :], ident), False)
            link0(v.tensor_copy(up_b[:, :], kc[:, K_UP:K_UP + P]), False)
            link0(v.tensor_copy(low_b[:, :], kc[:, K_LOW:K_LOW + P]), False)
            link0(v.tensor_copy(m1_b[:, :], kc[:, K_M1:K_M1 + FLASH]), False)
            hd = DB // 2
            for z in range(2):
                src = wqkv[:, z * C:(z + 1) * C].rearrange("c (h d) -> c d h", d=DB)
                link0(v.tensor_copy(wrot[:, 2 * z, :, :], src), False)
                link0(v.tensor_copy(wrot[:, 2 * z + 1, 0:hd, :], src[:, hd:DB, :]), False)
                link0(v.tensor_copy(wrot[:, 2 * z + 1, hd:DB, :], src[:, 0:hd, :]))
            n = 6 * C // QBLOCK
            g = wguR[:, :, :].rearrange("p a (b k) -> p (a b) k", k=QBLOCK)
            fp4(g, g, n, link0, link0)
            n = INNER_PAD // QBLOCK
            g = wdR[:, :].rearrange("p (b k) -> p b k", k=QBLOCK)
            fp4(g, g, n, link0, link0)
            dve.wait_ge(prep_pe, 15)
            link0(v.tensor_copy(wdT[:, :, :].rearrange("p a c -> p (a c)"), ps[:, 4, 0:3 * C]))
            assert count[0] == PREP_DVE, count[0]
            prep_over(dve)

            with dve.Fori(0, B) as i:
                steps = [0]

                def settle():
                    dve.wait_ge(dve_step, i * DVE_STEPS + steps[0])

                def link(ins, now=True):
                    steps[0] += 1
                    ins.then_inc(dve_step, 1)
                    if now:
                        settle()


                dve.wait_ge(x_loaded, i * PER["x_loaded"] + 16)
                layer_norm(xin, xn, link, lambda ins: ins.then_inc(xn_ready, 1))
                dve.wait_ge(xn_ready, i * PER["xn_ready"] + 4)
                layer_norm(xn, xh, link, lambda ins: ins.then_inc(xh_ready, 1))
                dve.wait_ge(h_ready, i * PER["h_ready"] + 1)
                link(v.tensor_scalar(hc[:, :], hpad[:, 2:T + 2], convw[:, 2:3], None, ALU.mult))
                link(v.scalar_tensor_tensor(out=hc[:, :], in0=hpad[:, 1:T + 1], scalar=convw[:, 1:2],
                                            in1=hc[:, :], op0=ALU.mult, op1=ALU.add))
                v.scalar_tensor_tensor(out=hc[:, :], in0=hpad[:, 0:T], scalar=convw[:, 0:1],
                                            in1=hc[:, :], op0=ALU.mult, op1=ALU.add).then_inc(conv_ready, 1)
                for z in range(2):
                    dve.wait_ge(qk_psum, i * PER["qk_psum"] + 2 * z + 2)
                    f, r = rope[:, 0, :], rope[:, 1, :]
                    link(v.tensor_tensor(f, ps[:, 2 + 2 * z, :], cosT, ALU.mult), False)
                    link(v.tensor_tensor(r, ps[:, 3 + 2 * z, :], sinT, ALU.mult))
                    link(v.tensor_tensor(f, f, r, ALU.add))
                    v.tensor_copy(part[:, z, 0, :], f).then_inc(split_ready, 1)
                    dve.wait_ge(split_ready, i * PER["split_ready"] + 3 * z + 1)
                    link(v.tensor_tensor(r, f, part[:, z, 0, :], ALU.subtract))
                    v.tensor_copy(part[:, z, 1, :], r).then_inc(split_ready, 1)
                    dve.wait_ge(split_ready, i * PER["split_ready"] + 3 * z + 2)
                    v.tensor_tensor(part[:, z, 2, :], r, part[:, z, 1, :],
                                                                    ALU.subtract).then_inc(split_ready, 1)
                    dve.wait_ge(split_ready, i * PER["split_ready"] + 3 * z + 3)
                for n in range(16):
                    g, t, b = n // 4, n % 4, 4 * (n % 2)
                    dve.wait_ge(bs_psum, i * PER["bs_psum"] + n + 1)
                    v.tensor_reduce(nmx[:, 4 * g:4 * g + 4, t], ps[:, b:b + 4, 0:P * (t + 1)], AX.X, ALU.max,
                                         negate=True).then_inc(bmax_ready, 1)
                dve.wait_ge(mxT_psum, i * PER["mxT_psum"] + 1)
                src = ps[0:HEADS * NT, 0, 0:P]
                v.tensor_copy(mx3[:, 0, :], src).then_inc(mx_split, 1)
                dve.wait_ge(mx_split, i * PER["mx_split"] + 1)
                link(v.tensor_tensor(mxr[:, :], src, mx3[:, 0, :], ALU.subtract))
                v.tensor_copy(mx3[:, 1, :], mxr[:, :]).then_inc(mx_split, 1)
                dve.wait_ge(mx_split, i * PER["mx_split"] + 2)
                v.tensor_tensor(mx3[:, 2, :], mxr[:, :], mx3[:, 1, :], ALU.subtract).then_inc(mx_split, 1)
                for t in range(NT):
                    dve.wait_ge(byT_psum, i * PER["byT_psum"] + t + 1)
                    y4 = ps[:, t, :].rearrange("p (h d) -> p h d", d=32)
                    link(v.reciprocal(rb[:, t, :], y4[:, :, DB]))
                    v.tensor_tensor(yn[:, t, :].rearrange("p (h d) -> p h d", d=DB), y4[:, :, 0:DB],
                                         rb[:, t, :].unsqueeze(2).to_broadcast([P, HEADS, DB]), ALU.mult)\
                                            .then_inc(yn_ready, 1)
                dve.wait_ge(bo_psum, i * PER["bo_psum"] + 1)
                flat = lambda a: a[:, :, :].rearrange("p t c -> p (t c)")
                link(v.tensor_tensor(flat(x1), flat(xn), ps[:, 5, :], ALU.add))
                layer_norm(x1, xh, link, lambda ins: ins.then_inc(xh2_ready, 1))
                dve.wait_ge(logits_psum, i * PER["logits_psum"] + 1)
                link(v.tensor_copy(flat(lg), ps[:, 7, 0:NT * EXPERTS]))
                link(v.tensor_reduce(lmax[:, :], lg[:, :, :], AX.X, ALU.max))
                link(v.tensor_tensor(lg[:, :, :], lg[:, :, :],
                                     lmax[:, :].unsqueeze(2).to_broadcast([P, NT, EXPERTS]), ALU.is_equal))
                link(v.tensor_copy(hot[:, :, 0], lg[:, :, 0]), False)
                link(v.tensor_copy(taken[:, :], lg[:, :, 0]))
                for e in range(1, EXPERTS):
                    link(v.tensor_tensor(hot[:, :, e], lg[:, :, e], taken[:, :], ALU.is_gt))
                    link(v.tensor_tensor(taken[:, :], taken[:, :], lg[:, :, e], ALU.max))

                def expert_y(n):
                    e, c = n // CHUNKS, n % CHUNKS
                    dve.wait_ge(silu_done, i * PER["silu_done"] + n + 1)
                    if e >= 2 and c == 0:
                        dve.wait_ge(down_psum, i * PER["down_psum"] + e - 1)
                    v.tensor_tensor(ym[:, e % 2, c, :], sg[:, n % 2, :], ps[:, 2 * (n % 3) + 1, :], ALU.mult)\
                       .then_inc(moe_y, 1)

                def expert_acc(e):
                    dve.wait_ge(down_psum, i * PER["down_psum"] + e + 1)
                    if e:
                        dve.wait_ge(moe_acc, i * PER["moe_acc"] + e)
                    for t in range(NT):
                        ins = v.scalar_tensor_tensor(out=x1[:, t, :], in0=ps[:, 6 + e % 2, t * P:(t + 1) * P],
                                                     scalar=hot[:, t, e:e + 1], in1=x1[:, t, :],
                                                     op0=ALU.mult, op1=ALU.add)
                        if t == NT - 1:
                            ins.then_inc(moe_acc, 1)
                        else:
                            link(ins, False)

                for n in range(16):
                    expert_y(n)
                    if n >= 6 and n % 4 == 2:
                        expert_acc(n // 4 - 1)
                expert_acc(3)
                dve.wait_ge(moe_acc, i * PER["moe_acc"] + 4)
                settle()
                link(v.tensor_tensor(flat(xp), flat(xin), flat(x1), ALU.add))

                def v_norm(h):
                    dve.wait_ge(aexp_done, i * PER["aexp_done"] + 4 * h + 4)
                    if h == 0:
                        dve.wait_ge(av_ready, i * PER["av_ready"] + 8)
                    if h >= 4:
                        dve.wait_ge(zav_done, i * PER["zav_done"] + (h - 4) // 2 + 1)
                    link(v.reciprocal(rla[:, h, :], la[:, h, :]))
                    v.tensor_tensor(vn[:, h % 4, :, :], va[:, :, h * DA:(h + 1) * DA],
                                         rla[:, h, :].unsqueeze(2).to_broadcast([P, NT, DA]), ALU.mult)\
                                            .then_inc(vn_ready, 1)

                for h in range(HEADS):
                    for t in range(NT):
                        dve.wait_ge(as_psum, i * PER["as_psum"] + 4 * h + t + 1)
                        v.tensor_reduce(nma[:, h, t:t + 1], ps[:, t, 0:P * (t + 1)], AX.X, ALU.max,
                                             negate=True).then_inc(amax, 1)
                    if h:
                        v_norm(h - 1)
                v_norm(HEADS - 1)
                dve.wait_ge(ao_psum, i * PER["ao_psum"] + 1)
                link(v.tensor_tensor(flat(xp), flat(xp), ps[:, 4, :], ALU.add))

                layer_norm(xp, xn, link, lambda ins: ins.then_inc(xn2_ready, 1))
                dve.wait_ge(kqv1_psum, i * PER["kqv1_psum"] + 3)
                link(v.tensor_tensor(v1[:, :, :], ps[:, 3, :].rearrange("p (t c) -> p t c", c=C),
                                     b1bc[:, 0, :].unsqueeze(1).to_broadcast([P, NT, C]), ALU.add), False)
                dve.wait_ge(kq1_ready, i * PER["kq1_ready"] + 2)
                v.tensor_tensor(qbd[:, :, :], q1T[:, :].unsqueeze(1).to_broadcast([C, HEADS, FLASH]),
                                     blk.unsqueeze(2).to_broadcast([C, HEADS, FLASH]), ALU.mult)\
                                        .then_inc(qbd_ready, 1)
                dve.wait_ge(xn2_ready, i * PER["xn2_ready"] + 4)
                k = lambda a: a[:, :, :].rearrange("p t (b k) -> p (t b) k", k=QBLOCK)
                fp4(k(xn), k(xq), NT * C // QBLOCK, link, lambda ins: ins.then_inc(xq_ready, 1))
                dve.wait_ge(s1_psum, i * PER["s1_psum"] + 1)
                s1 = ps[:, :, :].rearrange("p a (b k) -> p (a b) k", k=FLASH)
                ff = lambda a: a[:, :, :].rearrange("p a b -> p (a b)")
                link(v.tensor_reduce(ff(bm), s1, AX.X, ALU.max))
                link(v.tensor_copy(rm[:, :, 0], bm[:, :, 0]))
                for j in range(1, NFB):
                    link(v.tensor_tensor(rm[:, :, j], rm[:, :, j - 1], bm[:, :, j], ALU.max))
                wide = lambda a: ff(a).unsqueeze(2).to_broadcast([P, PAIRS * NFB, FLASH])
                s2 = ss[:, :, :, :].rearrange("p a b k -> p (a b) k")
                v.tensor_tensor(s2, s1, wide(rm), ALU.subtract).then_inc(sub1_ready, 1)
                v.tensor_tensor(dm[:, :, 1:NFB], rm[:, :, 0:NFB - 1], rm[:, :, 1:NFB], ALU.subtract)\
                   .then_inc(dm1_ready, 1)
                dve.wait_ge(p1_ready, i * PER["p1_ready"] + 1)
                link(v.tensor_reduce(ff(ll), s2, AX.X, ALU.add))
                dve.wait_ge(fac1_ready, i * PER["fac1_ready"] + 1)
                for j in range(1, NFB):
                    link(v.tensor_tensor(cc[:, :], ll[:, :, j - 1], dm[:, :, j], ALU.mult))
                    link(v.tensor_tensor(ll[:, :, j], ll[:, :, j], cc[:, :], ALU.add))
                link(v.reciprocal(ff(rl), ff(ll)))
                link(v.tensor_tensor(rr[:, :, 1:NFB], ll[:, :, 0:NFB - 1], rl[:, :, 1:NFB], ALU.mult), False)
                link(v.memset(rr[:, :, 0:1], 0.0), False)
                link(v.tensor_copy(cc[:, :], rl[:, :, NFB - 1]))
                link(v.tensor_scalar(dm[:, :, :], rr[:, :, :], -1.0, 1.0, ALU.mult, ALU.add))
                for j in range(NFB - 1, -1, -1):
                    link(v.tensor_tensor(co[:, :, j], rr[:, :, j], cc[:, :], ALU.mult))
                    if j:
                        link(v.tensor_tensor(cc[:, :], cc[:, :], dm[:, :, j], ALU.mult))
                v.tensor_tensor(s2, s2, wide(co), ALU.mult).then_inc(pw1_ready, 1)
                pT = share_i
                for n in range(1, 8, 2):
                    dve.wait_ge(pT1_psum, i * PER["pT1_psum"] + n + 1)
                    v.tensor_copy(pT[:, 512 * n:512 * n + 512], ps[:, n, :]).then_inc(pT1_dve, 1)
                dve.wait_ge(o1_psum, i * PER["o1_psum"] + 1)
                link(v.tensor_tensor(om[:, :, :], ps[:, 0:2, :].rearrange("p a (h q) -> p (a h) q", q=FLASH),
                                     blk.unsqueeze(2).to_broadcast([C, HEADS, FLASH]), ALU.mult))
                v.tensor_reduce(oT[:, :], om[:, :, :].rearrange("p h q -> p q h"), AX.X, ALU.add)\
                   .then_inc(oT1_ready, 1)
                for t in range(NT):
                    dve.wait_ge(sgf_done, i * PER["sgf_done"] + t + 1)
                    v.tensor_tensor(hf[:, t, :], sgf[:, t % 2, :], ps[:, 5 + 2 * (t % 2), 0:INNER], ALU.mult)\
                       .then_inc(hf_done, 1)
                dve.wait_ge(hf_done, i * PER["hf_done"] + 4)
                g = hf[:, :, :].rearrange("p t (b k) -> p (t b) k", k=QBLOCK)
                fp4(g, g, NT * INNER // QBLOCK, link, link)
                link(v.memset(hq[:, :, INNER:INNER_PAD], 0.0), False)
                settle()
                v.tensor_copy(hq[:, :, 0:INNER], hf[:, :, :]).then_inc(hq_ready, 1)
                link(v.tensor_tensor(xp[:, :, :], xp[:, :, :],
                                     b1bc[:, 1, :].unsqueeze(1).to_broadcast([P, NT, C]), ALU.add))
                dve.wait_ge(pr1_psum, i * PER["pr1_psum"] + 1)
                link(v.tensor_tensor(xp[P - FLASH:P, NT - 1, :], xp[P - FLASH:P, NT - 1, :],
                                     ps[P - FLASH:P, 2, 0:C], ALU.add))
                dve.wait_ge(dn_psum, i * PER["dn_psum"] + 1)
                v.tensor_tensor(flat(yout), flat(xp), ps[:, 4, :], ALU.add).then_inc(out_ready, 1)
                assert steps[0] == DVE_STEPS, steps[0]

        @block.tensor
        def _(pe):
            mm, tr = nc.tensor.matmul, nc.tensor.transpose

            pe.wait_ge(weights_loaded, 16 * PREP_LOADS)
            pe.wait_ge(prep_dve, 6)
            for g in range(4):
                for h in range(4 * g, 4 * g + 4):
                    ins = mm(ps[:, g, (h % 4) * C:(h % 4 + 1) * C], wkq[:, 1, h, :], wkq[:, 0, h, :],
                             start=True, stop=True)
                ins.then_inc(prep_pe, 1)
            for g in range(2):
                for k in range(4):
                    ins = tr(ps[:, 4 + g, k * C:(k + 1) * C], raw[:, 4 * g + k, :], ident)
                ins.then_inc(prep_pe, 1)
            for g in range(2):
                for k in range(4):
                    n = 4 * g + k
                    ins = tr(ps[:, 6 + g, k * C:(k + 1) * C], raw2[:, n * C:(n + 1) * C], ident)
                ins.then_inc(prep_pe, 1)
            pe.wait_ge(prep_act, 1)
            for k in range(4):
                ins = tr(ps[:, 0, k * C:(k + 1) * C], w1raw[:, k, :], ident)
            ins.then_inc(prep_pe, 1)
            pe.wait_ge(prep_act, 2)
            mm(ps[:, 1, 0:2 * C], ones[:, :], brow[:, :], start=True, stop=True).then_inc(prep_pe, 1)
            pe.wait_ge(prep_act, 5)
            pe.wait_ge(prep_dve, PREP_DVE - 1)
            for k in range(6):
                ins = tr(ps[:, 2 + k // 3, (k % 3) * C:(k % 3 + 1) * C], wguR[:, k, :], ident)
                if k % 3 == 2:
                    ins.then_inc(prep_pe, 1)
            for k in range(3):
                tr(ps[:, 4, k * C:(k + 1) * C], wdR[:, k * C:(k + 1) * C], ident).then_inc(prep_pe, 1)
            prep_over(pe)

            with pe.Fori(0, B) as i:
                tile = lambda t: slice(t * P, (t + 1) * P)

                def transpose_tiles(src, bank):
                    for t in range(NT):
                        ins = tr(ps[:, bank, tile(t)], src[:, t, :], ident)
                    return ins

                pe.wait_ge(xn_ready, i * PER["xn_ready"] + 4)
                transpose_tiles(xn, 0).then_inc(xnT_psum, 1)
                pe.wait_ge(xh_ready, i * PER["xh_ready"] + 4)
                transpose_tiles(xh, 1).then_inc(xhT_psum, 1)
                pe.wait_ge(conv_ready, i * PER["conv_ready"] + 1)
                for z in range(4):
                    mm(ps[:, 2 + z, :], wrot[:, z, :, :].rearrange("c d h -> c (d h)"), hc[:, :],
                            start=True, stop=True).then_inc(qk_psum, 1)
                for t in range(NT):
                    ins = mm(ps[:, 6, tile(t)], hc[:, tile(t)], wqkv[:, 2 * C:3 * C], start=True, stop=True)
                ins.then_inc(bv_psum, 1)

                pe.wait_ge(bv_ready, i * PER["bv_ready"] + 1)
                pe.wait_ge(stack_loaded, i * PER["stack_loaded"] + 16 * 18)
                for n in range(16):
                    g, t, b = n // 4, n % 4, 4 * (n % 2)
                    if n >= 2:
                        pe.wait_ge(bmax_ready, i * PER["bmax_ready"] + n - 1)
                    for k in range(4):
                        h = 4 * g + k
                        mm(ps[:, b + k, 0:P * (t + 1)], qst[0:SHIFT_ROW, h, tile(t)],
                           kst[0:SHIFT_ROW, h, 0:P * (t + 1)], start=True, stop=False)
                        ins = mm(ps[:, b + k, tile(t)], ident_b[:, :], up_b[:, :], start=False, stop=True)
                    ins.then_inc(bs_psum, 1)
                pe.wait_ge(bmax_ready, i * PER["bmax_ready"] + 16)
                tr(ps[:, 0, 0:P], nmx[:, :, :].rearrange("p h t -> p (h t)"), ident).then_inc(mxT_psum, 1)

                def b_scores(n):
                    g, j = n // 4, n % 4
                    for half in range(2):
                        m = 2 * n + half
                        b = 2 * (m % 3)
                        if m >= 3:
                            pe.wait_ge(bexp_done, i * PER["bexp_done"] + m - 2)
                        for k in range(2):
                            h = 4 * g + 2 * half + k
                            mm(ps[:, b + k, 0:T - j * P], kst[0:SHIFT_ROW + PARTS, h, tile(j)],
                               qst[0:SHIFT_ROW + PARTS, h, j * P:T], start=True, stop=False)
                            ins = mm(ps[:, b + k, 0:P], ident_b[:, :], low_b[:, :], start=False, stop=True)
                        ins.then_inc(bst_psum, 1)

                def b_values(n):
                    g, j = n // 4, n % 4
                    pe.wait_ge(bexp_done, i * PER["bexp_done"] + 2 * n + 2)
                    if g >= 2 and j == 0:
                        pe.wait_ge(by_ready, i * PER["by_ready"] + g - 1)
                    for k in range(4):
                        ins = mm(ps[32 * k:32 * k + 32, 6 + g % 2, j * P:T], vaug[:, j, 4 * g + k, :],
                                 pt[:, n % 2, k, 0:T - j * P], start=(j == 0), stop=(j == NT - 1))
                    ins.then_inc(bav_done, 1)

                pe.wait_ge(shift_loaded, i * PER["shift_loaded"] + 48)
                for n in range(16):
                    b_scores(n)
                    if n:
                        b_values(n - 1)
                b_values(15)
                pe.wait_ge(by_ready, i * PER["by_ready"] + 4)
                for t in range(NT):
                    for g in range(4):
                        ins = tr(ps[:, t, tile(g)], ys[:, g, tile(t)], ident)
                    ins.then_inc(byT_psum, 1)
                for t in range(NT):
                    pe.wait_ge(yn_ready, i * PER["yn_ready"] + t + 1)
                    ins = tr(ps[:, 4, tile(t)], yn[:, t, :], ident)
                ins.then_inc(ynT_psum, 1)
                pe.wait_ge(ynT_ready, i * PER["ynT_ready"] + 1)
                for t in range(NT):
                    ins = mm(ps[:, 5, tile(t)], ynT[:, tile(t)], wproj[:, :], start=True, stop=True)
                ins.then_inc(bo_psum, 1)

                pe.wait_ge(xh2_ready, i * PER["xh2_ready"] + 4)
                transpose_tiles(xh, 6).then_inc(xh2T_psum, 1)
                pe.wait_ge(h2T_ready, i * PER["h2T_ready"] + 1)
                for t in range(NT):
                    ins = mm(ps[:, 7, t * EXPERTS:(t + 1) * EXPERTS], h2T[:, tile(t)], wrt[:, :],
                             start=True, stop=True)
                ins.then_inc(logits_psum, 1)

                def gate_value(n):
                    e, c = n // CHUNKS, n % CHUNKS
                    if n >= 3:
                        pe.wait_ge(moe_y, i * PER["moe_y"] + n - 2)
                    for z in range(2):
                        f = z * DFF + c * P
                        ins = mm(ps[:, 2 * (n % 3) + z, :], wgv[:, e, f:f + P], h2T[:, :], start=True, stop=True)
                    ins.then_inc(gv_psum, 1)

                def down(e):
                    pe.wait_ge(moe_y, i * PER["moe_y"] + 4 * e + 4)
                    if e >= 2:
                        pe.wait_ge(moe_acc, i * PER["moe_acc"] + e - 1)
                    for t in range(NT):
                        for c in range(CHUNKS):
                            ins = mm(ps[:, 6 + e % 2, tile(t)], ym[:, e % 2, c, tile(t)], wdn[:, e, c, :],
                                     start=(c == 0), stop=(c == CHUNKS - 1))
                    ins.then_inc(down_psum, 1)

                for n in range(16):
                    gate_value(n)
                    if n >= 5 and n % 4 == 1:
                        down(n // 4 - 1)
                down(3)

                for n in range(8):
                    if n >= 4:
                        pe.wait_ge(av_ready, i * PER["av_ready"] + n - 3)
                    mm(ps[:, n % 4, :], xnT[:, tile(n // 2)], wvT[:, 512 * (n % 2):512 * (n % 2) + 512],
                            start=True, stop=True).then_inc(avp_psum, 1)
                pe.wait_ge(av_ready, i * PER["av_ready"] + 8)

                def key_side(h):
                    if h >= 2:
                        pe.wait_ge(g_ready, i * PER["g_ready"] + h - 1)
                    mm(ps[:, 4 + h % 2, :], mg[:, h, :], xnT[:, :], start=True, stop=True).then_inc(g_psum, 1)

                def scores(h):
                    pe.wait_ge(g_ready, i * PER["g_ready"] + h + 1)
                    for t in range(NT):
                        if h:
                            pe.wait_ge(aexp_done, i * PER["aexp_done"] + 4 * (h - 1) + t + 1)
                        mm(ps[:, t, 0:P * (t + 1)], xnT[:, tile(t)], gs[:, h % 2, 0:P * (t + 1)],
                           start=True, stop=False)
                        mm(ps[:, t, tile(t)], ident_b[:, :], up_b[:, :], start=False, stop=True).then_inc(as_psum, 1)

                def values(p):
                    pe.wait_ge(vn_ready, i * PER["vn_ready"] + 2 * p + 2)
                    if p >= 2:
                        pe.wait_ge(z_ready, i * PER["z_ready"] + p - 1)
                    if p < 2:
                        pe.wait_ge(moe_acc, i * PER["moe_acc"] + 4)
                    for t in range(NT - 1, -1, -1):
                        for k in range(2):
                            h = 2 * p + k
                            ins = mm(ps[DA * k:DA * k + DA, 6 + p % 2, 0:P * (t + 1)], vn[:, h % 4, t, :],
                                     pa[:, h % 4, OFF[t]:OFF[t] + P * (t + 1)], start=(t == NT - 1), stop=(t == 0))
                    ins.then_inc(zav_done, 1)

                key_side(0)
                for h in range(HEADS):
                    if h + 1 < HEADS:
                        key_side(h + 1)
                    scores(h)
                    if h >= 2 and h % 2 == 0:
                        values(h // 2 - 1)
                values(PAIRS - 1)
                pe.wait_ge(z_ready, i * PER["z_ready"] + PAIRS)
                for t in range(NT):
                    for p in range(PAIRS):
                        ins = mm(ps[:, 4, tile(t)], zT[:, p, tile(t)], woT[:, p, :],
                                 start=(p == 0), stop=(p == PAIRS - 1))
                ins.then_inc(ao_psum, 1)

                pe.wait_ge(xn2_ready, i * PER["xn2_ready"] + 4)
                transpose_tiles(xn, 0).then_inc(xn2T_psum, 1)
                pe.wait_ge(xn2T_ready, i * PER["xn2T_ready"] + 1)
                mm(ps[:, 1, :], w1T[:, 1, :], xnT[:, :], start=True, stop=True).then_inc(kqv1_psum, 1)
                mm(ps[:, 2, 0:FLASH], w1T[:, 0, :], xnT[:, T - FLASH:T], start=True, stop=True).then_inc(kqv1_psum, 1)
                for t in range(NT):
                    ins = mm(ps[:, 3, tile(t)], xnT[:, tile(t)], w1T[:, 2, :], start=True, stop=True)
                ins.then_inc(kqv1_psum, 1)
                pe.wait_ge(qbd_ready, i * PER["qbd_ready"] + 1)
                for p in range(PAIRS):
                    mm(ps[:, p, :], qbd[:, 2 * p:2 * p + 2, :].rearrange("c h q -> c (h q)"), k1T[:, :],
                       start=True, stop=False)
                    ins = mm(ps[:, p, T - FLASH:T], ident_b[:, :], m1_b[:, :], start=False, stop=True)
                ins.then_inc(s1_psum, 1)
                pe.wait_ge(pw1_ready, i * PER["pw1_ready"] + 1)
                for n in range(8):
                    kt, half = n // 2, n % 2
                    for k in range(4):
                        src = ss[:, 4 * half + k, 2 * kt:2 * kt + 2, :].rearrange("p b k -> p (b k)")
                        ins = tr(ps[:, n, tile(k)], src, ident)
                    ins.then_inc(pT1_psum, 1)
                pe.wait_ge(pT1_act, i * PER["pT1_act"] + 4)
                pe.wait_ge(pT1_dve, i * PER["pT1_dve"] + 4)
                pT = share_i
                for half in range(2):
                    for kt in range(NT):
                        n = 2 * kt + half
                        ins = mm(ps[:, half, :], v1[:, kt, :], pT[:, 512 * n:512 * n + 512],
                                 start=(kt == 0), stop=(kt == NT - 1))
                ins.then_inc(o1_psum, 1)
                pe.wait_ge(xq_ready, i * PER["xq_ready"] + 1)
                transpose_tiles(xq, 3).then_inc(xqT_psum, 1)
                pe.wait_ge(xqT_ready, i * PER["xqT_ready"] + 1)

                def gate_up(t):
                    if t >= 2:
                        pe.wait_ge(hf_done, i * PER["hf_done"] + t - 1)
                    for z in range(2):
                        ins = mm(ps[:, 4 + 2 * (t % 2) + z, 0:INNER], xqT[:, tile(t)], wguT[:, z, 0:INNER],
                                 start=True, stop=True)
                    ins.then_inc(gu_psum, 1)

                gate_up(0)
                gate_up(1)
                pe.wait_ge(oT1_ready, i * PER["oT1_ready"] + 1)
                mm(ps[P - FLASH:P, 2, 0:C], oT[:, :], w1T[:, 3, :], start=True, stop=True).then_inc(pr1_psum, 1)
                gate_up(2)
                gate_up(3)
                pe.wait_ge(hq_ready, i * PER["hq_ready"] + 1)
                for t in range(NT):
                    for k in range(3):
                        ins = tr(ps[:, HT_BANK[t], tile(k)], hq[:, t, tile(k)], ident)
                    ins.then_inc(hqT_psum, 1)
                pe.wait_ge(hqT_ready, i * PER["hqT_ready"] + 4)
                for t in range(NT):
                    for k in range(3):
                        ins = mm(ps[:, 4, tile(t)], hqT[:, t, k, :], wdT[:, k, :], start=(k == 0), stop=(k == 2))
                ins.then_inc(dn_psum, 1)



NAMES = ['L0_attn_x', 'L0_attn_W_K', 'L0_attn_W_Q', 'L0_attn_W_V', 'L0_attn_W_O', 'L0_ffn_ln1_w', 'L0_ffn_ln1_b',
         'L0_ffn_ln2_w', 'L0_ffn_ln2_b', 'L0_ffn_conv_w', 'L0_ffn_attn_w', 'L0_ffn_proj_w', 'L0_ffn_router_w',
         'L0_ffn_expert_wv', 'L0_ffn_expert_proj', 'L1_attn_qkv_w', 'L1_attn_qkv_b', 'L1_attn_proj_w',
         'L1_attn_proj_b', 'L1_ffn_w_gate', 'L1_ffn_w_up', 'L1_ffn_w_down']


def kernel(**inputs):
    import numpy as _np
    import concourse.bacc as _bacc
    from concourse.bass_utils import run_bass_kernel_spmd as _run

    nc = _bacc.Bacc("TRN2", target_bir_lowering=False, num_devices=1)
    arrays, aps = {}, {}
    for name in NAMES:
        a = _np.ascontiguousarray(inputs[name])
        arrays[f"in_{name}"] = a
        aps[name] = nc.dram_tensor(f"in_{name}", a.shape, F32, kind="ExternalInput").ap()
    arrays["in_constants"] = shape_constants()
    consts = nc.dram_tensor("in_constants", (P, K_END), F32, kind="ExternalInput").ap()
    shape = arrays["in_L0_attn_x"].shape
    out = nc.dram_tensor("out_0", shape, F32, kind="ExternalOutput").ap()
    build_layers(nc, aps, aps["L0_attn_x"], consts, out)
    r = _run(nc, [arrays], core_ids=[0])
    return r.results[0]["out_0"]
```

```python
from contextlib import ExitStack

import numpy as np

import concourse.bass as bass
from concourse import mybir

ALU = mybir.AluOpType
ACT = mybir.ActivationFunctionType
AX = mybir.AxisListType
F32 = mybir.dt.float32
BF16 = mybir.dt.bfloat16
I32 = mybir.dt.int32

P = 128
C = 128
T = 512
NT = T // P
HEADS = 16
DA = 64
DB = C // HEADS
EXPERTS = 4
DFF = 512
CHUNKS = DFF // P
INNER = 352
INNER_PAD = 384
QBLOCK = 16
FLASH = 64
NFB = T // FLASH
PAIRS = HEADS // 2
EPS = 1e-5
FP4_MAX = 6.0
MASKED = -1e30
SCALE_B = float(DB) ** -0.5
VCOLS = 2 * DB
PARTS = 3
SHIFT_ROW = 96
KS = PARTS * PARTS * DB
OFF = [sum(P * (u + 1) for u in range(t)) for t in range(NT)]
ROWLEN = sum(P * (u + 1) for u in range(NT))


K_ID = 0
K_UP = K_ID + P
K_LOW = K_UP + P
K_M1 = K_LOW + P
K_BLK = K_M1 + FLASH
K_COS = K_BLK + HEADS
K_SIN = K_COS + T
K_END = K_SIN + T


def shape_constants():
    k = np.zeros((P, K_END), np.float32)
    row, col = np.arange(P)[:, None], np.arange(P)[None, :]
    k[:, K_ID:K_ID + P] = row == col
    k[:, K_UP:K_UP + P] = np.where(col > row, np.float32(MASKED), 0)
    k[:, K_LOW:K_LOW + P] = np.where(row > col, np.float32(MASKED), 0)
    q, key = np.arange(P)[:, None] % FLASH, np.arange(FLASH)[None, :]
    k[:, K_M1:K_M1 + FLASH] = np.where(key > q, np.float32(MASKED), 0)
    k[:, K_BLK:K_BLK + HEADS] = np.arange(P)[:, None] // DB == np.arange(HEADS)[None, :]
    inv = (1.0 / 10000.0 ** (np.arange(0, DB, 2, dtype=np.float32) / np.float32(DB))).astype(np.float32)
    ang = np.arange(T, dtype=np.float32)[None, :] * inv[:, None]
    ang = np.concatenate([ang, ang], 0)
    sign = np.where(np.arange(DB) < DB // 2, -1.0, 1.0)[:, None]
    k[:, K_COS:K_COS + T] = np.repeat(np.cos(ang), HEADS, 0)
    k[:, K_SIN:K_SIN + T] = np.repeat(np.sin(ang) * sign, HEADS, 0)
    return k


DENSE = dict(
    carried=1, xnTd_ready=1, avp_psum=8, av_ready=8, g_psum=16, g_ready=16, as_psum=64, amax=64, aexp_done=64,
    vn_ready=16, zav_done=8, z_ready=8, ao_psum=1, h2Td_ready=1, gate_psum=16, value_psum=16, silu_done=16, gate_read=16, rl_ready=16,
    moe_y=16, down_psum=16, moe_acc=4, ao_added=1,
)
AHEAD = dict(
    x_loaded=16, xn_ready=4, xh_ready=4, xnT_psum=1, xhT_psum=1, xnT_ready=1, h_ready=1, conv_ready=1,
    qk_psum=4, rope_read=2, bv_psum=1, bv_ready=1, split_ready=6, stack_loaded=16 * 18, bs_psum=44, bmax_ready=44,
    mxT_psum=1, mx_split=3, shift_loaded=48, bst_psum=44, bexp_done=44, bav_done=16, by_ready=4,
    byT_psum=4, yn_ready=4, ynT_psum=1, ynT_ready=1, bo_psum=1, x1_ready=1, xh2_ready=4, xh2T_psum=1, h2T_ready=1,
    logits_psum=1, hot_ready=1,
)
BEHIND = dict(
    xn2_ready=4, xn2T_psum=1, xn2T_ready=1, kqv1_psum=3, kq1_ready=2, v1_ready=1, qbd_ready=1, s1_psum=8,
    s1_ready=8, sub1_ready=4, dm1_ready=1, fac1_ready=1, p1_ready=4, co_ready=1, pw1_ready=4, sum1_ready=4, totals_ready=1, ratios_ready=1, pT1_psum=8,
    pT1_ready=8, o1_psum=2, om_ready=2, oT1_ready=1, pr1_psum=1, pr1_added=1, xq_ready=1, xqT_psum=1, xqT_ready=1,
    gate1_psum=4, sgf_done=8, up1_psum=4, hf_done=4, hq_ready=4, hqT_psum=4, hqT_ready=4,
    dn_psum=1, out_ready=1, out_stored=16,
)
PREP_LOADS = 29
BLEND_STEPS = 27
AHEAD_STEPS = 89
BEHIND_STEPS = 116

WIDTH_HEADS = {P: 4, 2 * P: 2, 3 * P: 1, 4 * P: 1}
MAX_UNITS = [(t, h, WIDTH_HEADS[P * (t + 1)]) for g in range(4) for t in range(NT)
             for h in range(4 * g, 4 * g + 4, WIDTH_HEADS[P * (t + 1)])]
EXP_UNITS = [(j, h, WIDTH_HEADS[T - P * j]) for g in range(4) for j in range(NT)
             for h in range(4 * g, 4 * g + 4, WIDTH_HEADS[T - P * j])]
UNITS = len(MAX_UNITS)
EXP_END = {}
for _u, (_j, _h, _k) in enumerate(EXP_UNITS):
    EXP_END[(_h // 4, _j)] = _u + 1


BEHIND_PLACES = [
    (0, "ln2_stats"), (0, "ln2_root"), (1, "ln2_apply"), (2, "transpose2"), (3, "keys1"), (3, "queries1"), (4,
    "values1"), (4, "spread_queries1"), (5, "scores1", 0), (6, "scores1", 1), (7, "scores1", 2), (8,
    "scores1", 3), (9, "scores1", 4), (10, "scores1", 5), (10, "block_max1", 0), (12, "scores1", 6), (12,
    "scores1", 7), (13, "block_max1", 1), (15, "running_max1"), (17, "shift1", 0), (18, "shift1", 1), (19,
    "shift1", 2), (20, "shift1", 3), (20, "sum1", 0), (23, "sum1", 1), (25, "sum1", 2), (25, "sum1", 3), (25,
    "totals1", 1, 4), (28, "totals1", 4, 8), (30, "ratios1"), (30, "blend1", 7, 4), (33, "blend1", 3, 0), (33,
    "weigh1", 0), (36, "weigh1", 1), (36, "probs_T1", 0, 0), (38, "weigh1", 2), (38, "probs_T1", 0, 1), (39,
    "weigh1", 3), (39, "probs_T1", 0, 2), (41, "probs_T1", 0, 3), (42, "mix1", 0), (43, "probs_T1", 1, 0),
    (44, "probs_T1", 1, 1), (45, "probs_T1", 1, 2), (46, "probs_T1", 1, 3), (47, "mix1", 1), (51, "project1"),
    (51, "round_x", 0), (53, "round_x", 1), (58, "round_x", 2), (64, "round_x", 3), (64, "round_x", 4), (67,
    "transpose_xq"), (68, "gate1", 0), (69, "up1", 0), (69, "round_h", 0, 0), (70, "round_h", 0, 1), (70,
    "round_h", 0, 2), (70, "round_h", 0, 3), (71, "round_h", 0, 4), (75, "transpose_hq", 0), (76, "gate1", 1),
    (77, "up1", 1), (77, "round_h", 1, 0), (81, "round_h", 1, 1), (82, "round_h", 1, 2), (83, "round_h", 1,
    3), (83, "round_h", 1, 4), (87, "transpose_hq", 1), (88, "gate1", 2), (99, "up1", 2), (99, "round_h", 2,
    0), (99, "round_h", 2, 1), (101, "round_h", 2, 2), (105, "round_h", 2, 3), (105, "round_h", 2, 4), (106,
    "transpose_hq", 2), (108, "gate1", 3), (110, "up1", 3), (111, "round_h", 3, 0), (112, "round_h", 3, 1),
    (112, "round_h", 3, 2), (118, "round_h", 3, 3), (118, "round_h", 3, 4), (123, "transpose_hq", 3), (126,
    "down1"),
]
AHEAD_PLACES = [
    (0, "load_x"), (2, "ln0_stats"), (3, "ln0_root"), (3, "ln0_apply"), (5, "transpose0"), (5, "ln1_stats"),
    (5, "ln1_root"), (7, "ln1_apply"), (7, "transpose1"), (8, "conv"), (10, "project_q"), (10, "split_q"),
    (11, "project_k"), (12, "split_k"), (15, "project_v"), (21, "row_max", 0), (26, "row_max", 1), (26,
    "row_max", 2), (27, "row_max", 3), (28, "row_max", 4), (29, "row_max", 5), (31, "row_max", 6), (33,
    "row_max", 7), (34, "row_max", 8), (38, "row_max", 9), (38, "row_max", 10), (39, "row_max", 11), (39,
    "row_max", 12), (40, "row_max", 13), (41, "row_max", 14), (41, "row_max", 15), (42, "row_max", 16), (42,
    "row_max", 17), (43, "row_max", 18), (43, "row_max", 19), (44, "row_max", 20), (44, "row_max", 21), (46,
    "row_max", 22), (47, "row_max", 23), (48, "row_max", 24), (49, "row_max", 25), (51, "row_max", 26), (54,
    "row_max", 27), (55, "row_max", 28), (57, "row_max", 29), (57, "row_max", 30), (58, "row_max", 31), (59,
    "row_max", 32), (61, "row_max", 33), (61, "row_max", 34), (62, "row_max", 35), (62, "row_max", 36), (63,
    "row_max", 37), (63, "row_max", 38), (63, "row_max", 39), (64, "row_max", 40), (64, "row_max", 41), (65,
    "row_max", 42), (68, "row_max", 43), (69, "shift_rows"), (70, "exps", 0), (71, "exps", 1), (72, "exps",
    2), (72, "exps", 3), (73, "exps", 4), (73, "attend", 0, 0), (74, "exps", 5), (74, "exps", 6), (76, "exps",
    7), (77, "exps", 8), (78, "exps", 9), (78, "attend", 0, 1), (78, "exps", 10), (78, "attend", 0, 2), (78,
    "exps", 11), (78, "attend", 0, 3), (79, "exps", 12), (80, "exps", 13), (80, "exps", 14), (81, "exps", 15),
    (81, "exps", 16), (81, "attend", 1, 0), (84, "exps", 17), (84, "exps", 18), (85, "exps", 19), (85,
    "attend", 1, 1), (86, "exps", 20), (86, "exps", 21), (87, "attend", 1, 2), (89, "exps", 22), (92, "exps",
    23), (93, "attend", 1, 3), (93, "exps", 24), (94, "exps", 25), (96, "exps", 26), (98, "attend", 2, 0),
    (98, "exps", 27), (98, "exps", 28), (99, "exps", 29), (102, "exps", 30), (105, "exps", 31), (105,
    "attend", 2, 1), (105, "exps", 32), (105, "attend", 2, 2), (105, "exps", 33), (105, "attend", 2, 3), (106,
    "exps", 34), (106, "exps", 35), (109, "exps", 36), (110, "exps", 37), (110, "exps", 38), (112, "attend",
    3, 0), (112, "exps", 39), (112, "exps", 40), (114, "exps", 41), (114, "attend", 3, 1), (115, "exps", 42),
    (116, "exps", 43), (116, "attend", 3, 2), (116, "attend", 3, 3), (119, "divide", 0), (119, "divide", 1),
    (120, "divide", 2), (120, "divide", 3), (123, "join"), (124, "project_y"), (124, "ln3_stats"), (126,
    "ln3_root"), (126, "ln3_apply"), (127, "transpose3"), (127, "route"),
]


def side_schedule():
    at = [[] for _ in range(8 * HEADS)]
    for places in (BEHIND_PLACES, AHEAD_PLACES):
        for place, *step in places:
            at[place].append(step)
    return at


SIDE = side_schedule()
BEHIND_NAMES = {"ln2_stats", "ln2_root", "ln2_apply", "transpose2", "keys1", "queries1", "values1",
                "spread_queries1", "scores1", "block_max1", "running_max1", "shift1", "sum1", "totals1", "ratios1",
                "blend1", "weigh1", "probs_T1", "mix1", "project1", "round_x", "transpose_xq", "gate1", "up1",
                "round_h", "transpose_hq", "down1"}


def counter(eng, name=None):
    value = eng.alloc_register(name) if name else None

    def count(seq, each, n):
        reg, more = seq
        if value is None or type(reg) is int or more * each + n == 0:
            return reg * each + (more * each + n)
        eng.reg_add(value, reg * each, more * each + n)
        return value

    return count


def walk(steps, dense, i, nxt, prv):
    for pos, side in enumerate(SIDE):
        if i is not None:
            dense(pos)
        for name, *args in side:
            if name in steps and (prv if name in BEHIND_NAMES else nxt) is not None:
                steps[name](*args)


def build_layers(nc, w, x, consts, out):
    B = x.shape[0]
    with ExitStack() as ctx:
        def sb(name, shape, dt=F32):
            return ctx.enter_context(nc.sbuf_tensor(name, shape, dt))

        def sem(name):
            return ctx.enter_context(nc.semaphore(name))

        def view(buf, shape, at=0, dt=F32):
            n = int(np.prod(shape[1:])) * (2 if dt == BF16 else 4) // 4
            a = buf[0:shape[0], at:at + n]
            if dt != F32:
                a = a.bitcast(dt)
            if len(shape) == 2:
                return a
            names = "abcd"[:len(shape) - 1]
            return a.rearrange(f"p ({' '.join(names)}) -> p {' '.join(names)}",
                               **dict(zip(names[1:], shape[2:])))

        share_a = sb("share_a", [P, 4 * ROWLEN])
        share_z = sb("share_z", [P, 4096])
        share_g = sb("share_g", [P, 1024])
        share_r = sb("share_r", [P, 2560])
        share_h = sb("share_h", [P, T])
        share_s = sb("share_s", [P, 6144])
        share_q = sb("share_q", [P, 1024])

        ident = sb("ident", [P, P])
        ident_b = sb("ident_b", [P, P], BF16)
        up_b = sb("up_b", [P, P], BF16)
        low_b = sb("low_b", [P, P], BF16)
        m1_b = sb("m1_b", [P, FLASH], BF16)
        tab = sb("tab", [P, K_END - K_BLK])
        blk = tab[:, 0:HEADS]
        cosT, sinT = tab[:, K_COS - K_BLK:K_COS - K_BLK + T], tab[:, K_SIN - K_BLK:K_SIN - K_BLK + T]
        masks = view(share_r, [P, K_BLK - K_UP])
        wkq = view(share_a, [DA, 2, HEADS, C])
        raw = view(share_z, [P, 8, C])
        raw2 = view(share_z, [P, 8 * C], 1024)
        w1raw = view(share_z, [P, 4, C], 2048)
        wqkraw = view(share_z, [C, 2 * C], 2560)
        wguR = view(share_z, [P, 6, C], 2816)
        wdR = view(share_z, [P, INNER_PAD], 3584)
        mg = sb("mg", [P, HEADS, C])
        wvT = sb("wvT", [C, HEADS * DA])
        woT = sb("woT", [P, PAIRS, C])
        ln1 = sb("ln1", [C, 4])
        convw = sb("convw", [C, 3])
        wbv = sb("wbv", [C, C])
        wrot = sb("wrot", [C, 4, DB, HEADS])
        wproj = sb("wproj", [C, C])
        wrt = sb("wrt", [C, EXPERTS])
        wgv = sb("wgv", [C, EXPERTS, 2 * DFF])
        wdn = sb("wdn", [P, EXPERTS, CHUNKS, C])
        w1T = sb("w1T", [C, 4, C])
        b1col = sb("b1col", [P, 2])
        brow = view(share_h, [1, 2 * C])
        ones = view(share_h, [1, P], 2 * C)
        b1bc = sb("b1bc", [P, 2, C])
        wguT = sb("wguT", [C, 2, INNER])
        wdT = sb("wdT", [P, 3, C])

        xnTd = sb("xnTd", [C, T])
        h2Td = sb("h2Td", [C, T])
        xacc = sb("xacc", [P, NT, C])
        hotd = sb("hotd", [P, NT, EXPERTS])
        va = sb("va", [P, 2, NT, 2 * DA])
        gs = view(share_g, [P, 2, T])
        nma = sb("nma", [P, HEADS, NT])
        la = sb("la", [P, HEADS, NT])
        rla = sb("rla", [P, HEADS, NT])
        pa = view(share_a, [P, 4, ROWLEN])
        vn = sb("vn", [P, 4, NT, DA])
        zT = view(share_z, [P, PAIRS, T])
        sg = view(share_g, [P, 2, T])
        ym = view(share_a, [P, 2, CHUNKS, T])

        xin = sb("xin", [P, NT, C])
        xn = sb("xn", [P, NT, C])
        xh = sb("xh", [P, NT, C])
        xnT = sb("xnT", [C, T])
        hpad = sb("hpad", [C, T + 2])
        hc = view(share_h, [C, T])
        rope = view(share_r, [P, 2, T])
        part = view(share_r, [P, 2, PARTS, T], 1024, BF16)
        kst = sb("kst", [P, HEADS, T], BF16)
        qst = sb("qst", [P, HEADS, T], BF16)
        vones = sb("vones", [P, (NT * HEADS + 1) * VCOLS])
        vaug = vones[:, 0:NT * HEADS * VCOLS].rearrange("p (t h d) -> p t h d", h=HEADS, d=VCOLS)
        nmx = sb("nmx", [P, 2 * HEADS, NT])
        mx3 = view(share_h, [HEADS * NT, PARTS, P], 0, BF16)
        mxr = view(share_h, [HEADS * NT, P], 256)
        pt = view(share_z, [P, 2, 4, T])
        ys = view(share_r, [P, 4, T])
        rb = sb("rb", [P, NT, HEADS])
        yn = view(share_r, [P, NT, C], 2048)
        ynT = view(share_h, [C, T])
        x1 = view(share_r, [P, NT, C])
        h2T = view(share_h, [C, T])
        lg = sb("lg", [P, NT, EXPERTS])
        lmax = sb("lmax", [P, NT])
        hot = sb("hot", [P, NT, EXPERTS])
        taken = sb("taken", [P, NT])

        xp = sb("xp", [P, NT, C])
        xn2 = sb("xn2", [P, NT, C])
        xn2T = view(share_s, [C, T], 5120)
        k1T = view(share_q, [C, T])
        v1 = view(share_q, [P, NT, C], T)
        q1T = sb("q1T", [C, FLASH])
        ss = view(share_s, [P, PAIRS, NFB, FLASH])
        om = view(share_s, [C, HEADS, FLASH])
        qbd = view(share_s, [C, HEADS, FLASH], 4096)
        pT = view(share_s, [P, NT, T], 4096)
        bm = sb("bm", [P, PAIRS, NFB])
        rm = sb("rm", [P, PAIRS, NFB])
        dm = sb("dm", [P, PAIRS, NFB])
        ll = sb("ll", [P, PAIRS, NFB])
        rl = sb("rl", [P, PAIRS, NFB])
        rr = sb("rr", [P, PAIRS, NFB])
        co = sb("co", [P, PAIRS, NFB])
        cc = sb("cc", [P, PAIRS])
        oT = sb("oT", [C, FLASH])
        NQ = C * NT // QBLOCK
        QS = NQ * QBLOCK
        qa, qc, qd, qe = (view(share_s, [P, NQ, QBLOCK], 1024 + k * QS) for k in range(4))
        xq = view(share_s, [P, NT, C], 3072)
        xqT = view(share_s, [C, T], 3584)
        sgf = view(share_s, [P, INNER], INNER)
        hf = view(share_s, [P, INNER])
        hq = view(share_q, [P, 2, INNER_PAD])
        hqT = view(share_s, [P, NT, 3 * P], 4096)
        yout = xn2
        qm = sb("qm", [P, 48])
        qr = sb("qr", [P, 48])

        norm_scratch = [[sb(f"{n}{k}", shape, dt) for n, shape, dt in (
            ("st", [P, NT, 6], F32), ("mv", [P, 3, NT], F32), ("ve", [P, NT], F32), ("ri", [P, NT], I32),
            ("ry", [P, NT], F32), ("rt", [P, NT], F32))] for k in range(2)]

        ps = ctx.enter_context(nc.psum_tensor("ps", [P, 8, 512], F32))

        carried = sem("carried")
        xnTd_ready = sem("xnTd_ready")
        avp_psum = sem("avp_psum")
        av_ready = sem("av_ready")
        g_psum = sem("g_psum")
        g_ready = sem("g_ready")
        as_psum = sem("as_psum")
        amax = sem("amax")
        aexp_done = sem("aexp_done")
        vn_ready = sem("vn_ready")
        zav_done = sem("zav_done")
        z_ready = sem("z_ready")
        ao_psum = sem("ao_psum")
        h2Td_ready = sem("h2Td_ready")
        gate_psum = sem("gate_psum")
        value_psum = sem("value_psum")
        silu_done = sem("silu_done")
        gate_read = sem("gate_read")
        rl_ready = sem("rl_ready")
        moe_y = sem("moe_y")
        down_psum = sem("down_psum")
        moe_acc = sem("moe_acc")
        ao_added = sem("ao_added")
        x_loaded = sem("x_loaded")
        xn_ready = sem("xn_ready")
        xh_ready = sem("xh_ready")
        xnT_psum = sem("xnT_psum")
        xhT_psum = sem("xhT_psum")
        xnT_ready = sem("xnT_ready")
        h_ready = sem("h_ready")
        conv_ready = sem("conv_ready")
        qk_psum = sem("qk_psum")
        rope_read = sem("rope_read")
        bv_psum = sem("bv_psum")
        bv_ready = sem("bv_ready")
        split_ready = sem("split_ready")
        stack_loaded = sem("stack_loaded")
        bs_psum = sem("bs_psum")
        bmax_ready = sem("bmax_ready")
        mxT_psum = sem("mxT_psum")
        mx_split = sem("mx_split")
        shift_loaded = sem("shift_loaded")
        bst_psum = sem("bst_psum")
        bexp_done = sem("bexp_done")
        bav_done = sem("bav_done")
        by_ready = sem("by_ready")
        byT_psum = sem("byT_psum")
        yn_ready = sem("yn_ready")
        ynT_psum = sem("ynT_psum")
        ynT_ready = sem("ynT_ready")
        bo_psum = sem("bo_psum")
        x1_ready = sem("x1_ready")
        xh2_ready = sem("xh2_ready")
        xh2T_psum = sem("xh2T_psum")
        h2T_ready = sem("h2T_ready")
        logits_psum = sem("logits_psum")
        hot_ready = sem("hot_ready")
        xn2_ready = sem("xn2_ready")
        xn2T_psum = sem("xn2T_psum")
        xn2T_ready = sem("xn2T_ready")
        kqv1_psum = sem("kqv1_psum")
        kq1_ready = sem("kq1_ready")
        v1_ready = sem("v1_ready")
        qbd_ready = sem("qbd_ready")
        s1_psum = sem("s1_psum")
        s1_ready = sem("s1_ready")
        sub1_ready = sem("sub1_ready")
        dm1_ready = sem("dm1_ready")
        fac1_ready = sem("fac1_ready")
        p1_ready = sem("p1_ready")
        co_ready = sem("co_ready")
        pw1_ready = sem("pw1_ready")
        sum1_ready = sem("sum1_ready")
        totals_ready = sem("totals_ready")
        ratios_ready = sem("ratios_ready")
        pT1_psum = sem("pT1_psum")
        pT1_ready = sem("pT1_ready")
        o1_psum = sem("o1_psum")
        om_ready = sem("om_ready")
        oT1_ready = sem("oT1_ready")
        pr1_psum = sem("pr1_psum")
        pr1_added = sem("pr1_added")
        xq_ready = sem("xq_ready")
        xqT_psum = sem("xqT_psum")
        xqT_ready = sem("xqT_ready")
        gate1_psum = sem("gate1_psum")
        sgf_done = sem("sgf_done")
        up1_psum = sem("up1_psum")
        hf_done = sem("hf_done")
        hq_ready = sem("hq_ready")
        hqT_psum = sem("hqT_psum")
        hqT_ready = sem("hqT_ready")
        dn_psum = sem("dn_psum")
        out_ready = sem("out_ready")
        out_stored = sem("out_stored")
        weights_loaded = sem("weights_loaded")
        prep_pe = sem("prep_pe")
        prep_act = sem("prep_act")
        prep_dve = sem("prep_dve")
        ahead_step = sem("ahead_step")
        behind_step = sem("behind_step")
        blend_step = sem("blend_step")

        block = ctx.enter_context(nc.Block())

        PREP_DVE = 52
        PREP_PE = 15
        PREP_ACT = 11

        def prep_over(eng):
            eng.wait_ge(prep_dve, PREP_DVE)
            eng.wait_ge(prep_act, PREP_ACT)

        def pipeline(eng, run):
            run(None, (0, 0), None)
            run((0, 0), (0, 1), None)
            with eng.Fori(1, B - 1) as i:
                run((i, 0), (i, 1), (i, -1))
            run((0, B - 1), None, (0, B - 2))
            run(None, None, (0, B - 1))

        @block.sync
        def _(sp):
            count = counter(sp)
            col = lambda a: a.rearrange("(p a) -> p a", a=1)
            cut = INNER - 2 * P
            loads = [
                (ident[:, :], consts[:, K_ID:K_ID + P]),
                (masks, consts[:, K_UP:K_BLK]),
                (tab[:, :], consts[:, K_BLK:K_END]),
                (wkq[:, 0], w["L0_attn_W_K"].rearrange("a h e -> h a e")),
                (wkq[:, 1], w["L0_attn_W_Q"].rearrange("a h e -> h a e")),
                (raw, w["L0_attn_W_V"].rearrange("(n a) h e -> (a h) n e", a=2)),
                (raw2, w["L0_attn_W_O"]),
                (ln1[:, 0:1], col(w["L0_ffn_ln1_w"])), (ln1[:, 1:2], col(w["L0_ffn_ln1_b"])),
                (ln1[:, 2:3], col(w["L0_ffn_ln2_w"])), (ln1[:, 3:4], col(w["L0_ffn_ln2_b"])),
                (convw[:, :], w["L0_ffn_conv_w"].rearrange("c a k -> c (a k)")),
                (wqkraw, w["L0_ffn_attn_w"][:, 0:2 * C]),
                (wbv[:, :], w["L0_ffn_attn_w"][:, 2 * C:3 * C]),
                (wproj[:, :], w["L0_ffn_proj_w"]),
                (wrt[:, :], w["L0_ffn_router_w"]),
                (wgv[:, :, :], w["L0_ffn_expert_wv"].rearrange("e c f -> c e f")),
                (wdn[:, :, :, :], w["L0_ffn_expert_proj"].rearrange("e (k p) c -> p e k c", p=P)),
                (w1raw[:, 0:3, :], w["L1_attn_qkv_w"].rearrange("(n p) c -> p n c", p=P)),
                (w1raw[:, 3, :], w["L1_attn_proj_w"]),
                (b1col[:, 0:1], col(w["L1_attn_qkv_b"][0:C])),
                (b1col[:, 1:2], col(w["L1_attn_qkv_b"][C:2 * C])),
                (brow[:, 0:C], w["L1_attn_qkv_b"][2 * C:3 * C].rearrange("(a c) -> a c", a=1)),
                (brow[:, C:2 * C], w["L1_attn_proj_b"].rearrange("(a c) -> a c", a=1)),
            ]
            for dst, src in loads:
                sp.dma_start(dst, src).then_inc(weights_loaded, 16)
            sp.wait_ge(prep_dve, 2)
            for n, name in enumerate(("L1_ffn_w_gate", "L1_ffn_w_up")):
                sp.dma_start(wguR[:, 3 * n:3 * n + 2, :],
                             w[name][0:2 * P, :].rearrange("(n p) c -> p n c", p=P)).then_inc(weights_loaded, 16)
                sp.dma_start(wguR[0:cut, 3 * n + 2, :], w[name][2 * P:INNER, :]).then_inc(weights_loaded, 16)
            sp.dma_start(wdR[:, 0:INNER], w["L1_ffn_w_down"]).then_inc(weights_loaded, 16)
            assert len(loads) + 5 == PREP_LOADS, len(loads)
            prep_over(sp)

            def run(i, nxt, prv):
                if nxt is None:
                    return
                for z, stack in ((0, qst), (1, kst)):
                    for a in range(PARTS):
                        sp.wait_ge(split_ready, count(nxt, AHEAD["split_ready"], 3 * z + a + 1))
                        for b in range(PARTS):
                            r = DB * (PARTS * a + b) if z == 0 else DB * (PARTS * b + a)
                            sp.dma_start(stack[r:r + DB, :, :], part[:, z, a, :]).then_inc(stack_loaded, 16)
                for a in range(PARTS):
                    sp.wait_ge(mx_split, count(nxt, AHEAD["mx_split"], a + 1))
                    sp.dma_start(qst[SHIFT_ROW + a:SHIFT_ROW + a + 1, :, :].rearrange(
                        "o h (t q) -> o (h t) q", t=NT), mx3[:, a, :]).then_inc(shift_loaded, 16)

            pipeline(sp, run)

        @block.gpsimd
        def _(pool):
            count = counter(pool)
            def run(i, nxt, prv):
                steps_done = [0]

                def link(ins):
                    steps_done[0] += 1
                    ins.then_inc(blend_step, 1)
                    pool.wait_ge(blend_step, count(prv, BLEND_STEPS, steps_done[0]))

                def normalise(h):
                    pool.wait_ge(av_ready, count(i, DENSE["av_ready"], h // 2 + 1))
                    if h >= 4:
                        pool.wait_ge(zav_done, count(i, DENSE["zav_done"], (h - 4) // 2 + 1))
                    pool.wait_ge(rl_ready, count(i, DENSE["rl_ready"], h + 1))
                    nc.gpsimd.tensor_tensor(vn[:, h % 4, :, :],
                                                 va[:, h // 2 % 2, :, (h % 2) * DA:(h % 2 + 1) * DA],
                                                 rla[:, h, :].unsqueeze(2).to_broadcast([P, NT, DA]), ALU.mult)\
                                                    .then_inc(vn_ready, 1)

                def dense(pos):
                    h, t = pos // 4, pos % 4
                    if 0 < h < HEADS and t == 1:
                        normalise(h - 1)
                    if h == HEADS and t == 0:
                        normalise(HEADS - 1)

                def spread_queries1():
                    pool.wait_ge(kq1_ready, count(prv, BEHIND["kq1_ready"], 2))
                    nc.gpsimd.tensor_tensor(qbd, q1T[:, :].unsqueeze(1).to_broadcast([C, HEADS, FLASH]),
                                                 blk.unsqueeze(2).to_broadcast([C, HEADS, FLASH]), ALU.mult)\
                                                    .then_inc(qbd_ready, 1)

                def totals1(a, b):
                    pool.wait_ge(fac1_ready, count(prv, BEHIND["fac1_ready"], 1))
                    pool.wait_ge(sum1_ready, count(prv, BEHIND["sum1_ready"], 4))
                    for j in range(a, b):
                        link(nc.gpsimd.tensor_tensor(cc[:, :], ll[:, :, j - 1], dm[:, :, j], ALU.mult))
                        ins = nc.gpsimd.tensor_tensor(ll[:, :, j], ll[:, :, j], cc[:, :], ALU.add)
                        if j < NFB - 1:
                            link(ins)
                        else:
                            ins.then_inc(totals_ready, 1)

                def blend1(a, b):
                    pool.wait_ge(ratios_ready, count(prv, BEHIND["ratios_ready"], 1))
                    for j in range(a, b - 1, -1):
                        ins = nc.gpsimd.tensor_tensor(co[:, :, j], rr[:, :, j], cc[:, :], ALU.mult)
                        if j:
                            link(ins)
                            link(nc.gpsimd.tensor_tensor(cc[:, :], cc[:, :], dm[:, :, j], ALU.mult))
                        else:
                            ins.then_inc(co_ready, 1)

                def weigh1(k):
                    pool.wait_ge(co_ready, count(prv, BEHIND["co_ready"], 1))
                    two = ss[:, 2 * k:2 * k + 2, :, :].rearrange("p a b k -> p (a b) k")
                    weight = co[:, 2 * k:2 * k + 2, :].rearrange("p a b -> p (a b)")
                    nc.gpsimd.tensor_tensor(two, two, weight.unsqueeze(2).to_broadcast(
                        [P, 2 * NFB, FLASH]), ALU.mult).then_inc(pw1_ready, 1)

                walk(dict(spread_queries1=spread_queries1, totals1=totals1,
                          blend1=blend1, weigh1=weigh1), dense, i, nxt, prv)
                assert prv is None or steps_done[0] == BLEND_STEPS, (steps_done[0], "BLEND_STEPS")

            prep_over(pool)
            pipeline(pool, run)

        @block.scalar
        def _(act):
            count = counter(act, "act_wait")
            copy = nc.scalar.copy
            activation = nc.scalar.activation

            def evac(n, dst, src, scale=1.0):
                act.wait_ge(prep_pe, n)
                activation(dst, src, ACT.Copy, scale=scale).then_inc(prep_act, 1)

            for g in range(4):
                evac(g + 1, mg[:, 4 * g:4 * g + 4, :].rearrange("p h c -> p (h c)"), ps[:, g, :], DA ** -0.5)
            for g in range(2):
                evac(5 + g, wvT[:, 512 * g:512 * g + 512], ps[:, 4 + g, :])
            for g in range(2):
                evac(7 + g, woT[:, 4 * g:4 * g + 4, :].rearrange("p h c -> p (h c)"), ps[:, 6 + g, :])
            evac(9, w1T[:, :, :].rearrange("p h c -> p (h c)"), ps[:, 0, :])
            evac(10, b1bc[:, :, :].rearrange("p h c -> p (h c)"), ps[:, 1, 0:2 * C])
            evac(15, wguT[:, :, :], ps[:, 2:4, 0:INNER])
            prep_over(act)

            def run(i, nxt, prv):
                def carry():
                    act.wait_ge(xnT_ready, count(i, AHEAD["xnT_ready"], 1))
                    copy(xnTd[:, :], xnT[:, :]).then_inc(xnTd_ready, 1)
                    if prv is not None:
                        act.wait_ge(down_psum, count(prv, DENSE["down_psum"], NT * EXPERTS))
                    act.wait_ge(h2T_ready, count(i, AHEAD["h2T_ready"], 1))
                    copy(h2Td[:, :], h2T[:, :]).then_inc(h2Td_ready, 1)

                def v_evac(p):
                    act.wait_ge(avp_psum, count(i, DENSE["avp_psum"], p + 1))
                    if p >= 2:
                        act.wait_ge(vn_ready, count(i, DENSE["vn_ready"], 2 * p - 2))
                    copy(va[:, p % 2, :, :].rearrange("p t c -> p (t c)"), ps[:, 3, :]).then_inc(av_ready, 1)

                def g_evac(h):
                    act.wait_ge(g_psum, count(i, DENSE["g_psum"], h + 1))
                    if h >= 2:
                        act.wait_ge(as_psum, count(i, DENSE["as_psum"], 4 * (h - 1)))
                    copy(gs[:, h % 2, :], ps[:, 3, :]).then_inc(g_ready, 1)

                def z_evac(p):
                    act.wait_ge(zav_done, count(i, DENSE["zav_done"], p + 1))
                    copy(zT[:, p, :], ps[:, 4, :]).then_inc(z_ready, 1)

                def dense(pos):
                    h, t = pos // 4, pos % 4
                    if pos == 0:
                        carry()
                        v_evac(0)
                        g_evac(0)
                    if h < HEADS:
                        if t == 0 and h % 2 and h + 1 < HEADS:
                            v_evac((h + 1) // 2)
                        if t == 2 and h + 1 < HEADS:
                            g_evac(h + 1)
                        if h >= 4 and t == 0:
                            act.wait_ge(zav_done, count(i, DENSE["zav_done"], (h - 4) // 2 + 1))
                        act.wait_ge(amax, count(i, DENSE["amax"], pos + 1))
                        activation(pa[:, h % 4, OFF[t]:OFF[t] + P * (t + 1)], ps[:, pos % 3, 0:P * (t + 1)],
                                        ACT.Exp, bias=nma[:, h, t:t + 1], accum_out=la[:, h, t:t + 1])\
                                           .then_inc(aexp_done, 1)
                        if t == 3 and h % 2 and h >= 3:
                            z_evac((h - 3) // 2)
                        return
                    n = h - HEADS
                    if n == 0 and t == 0:
                        z_evac(PAIRS - 1)
                    if t == 1:
                        act.wait_ge(gate_psum, count(i, DENSE["gate_psum"], n + 1))
                        if n >= 2:
                            act.wait_ge(moe_y, count(i, DENSE["moe_y"], n - 1))
                        activation(sg[:, n % 2, :], ps[:, (2 * n) % 3, :], ACT.Tanh, scale=0.5).then_inc(silu_done, 1)

                def load_x():
                    if i is not None:
                        act.wait_ge(carried, count(i, DENSE["carried"], 1))
                    act.dma_start(xin[:, :, :], x[bass.ds(nxt[0] + nxt[1], 1), :, :].rearrange(
                        "a (t p) c -> p (a t) c", p=P)).then_inc(x_loaded, 16)

                def transpose0():
                    act.wait_ge(xnT_psum, count(nxt, AHEAD["xnT_psum"], 1))
                    copy(xnT[:, :], ps[:, 5, :]).then_inc(xnT_ready, 1)

                def transpose1():
                    act.wait_ge(xhT_psum, count(nxt, AHEAD["xhT_psum"], 1))
                    activation(hpad[:, 2:T + 2], ps[:, 6, :], ACT.Identity, bias=ln1[:, 1:2],
                                    scale=ln1[:, 0:1]).then_inc(h_ready, 1)

                def project_v():
                    act.wait_ge(bv_psum, count(nxt, AHEAD["bv_psum"], 1))
                    copy(vaug[:, :, :, 0:DB].rearrange("p t h d -> p (t h) d"),
                              ps[:, 5, :].rearrange("p (n d) -> p n d", d=DB)).then_inc(bv_ready, 1)

                def exps(u):
                    j, h, k = EXP_UNITS[u]
                    n, wd = h // 4 * NT + j, T - P * j
                    if u == 0 and i is not None:
                        act.wait_ge(ao_psum, count(i, DENSE["ao_psum"], 1))
                    if n >= 2 and h % 4 == 0:
                        act.wait_ge(bav_done, count(nxt, AHEAD["bav_done"], n - 1))
                    act.wait_ge(bst_psum, count(nxt, AHEAD["bst_psum"], u + 1))
                    src = ps[:, 5 + u % 2, 0:k * wd].rearrange("p (k w) -> p k w", w=wd)
                    activation(pt[:, n % 2, h % 4:h % 4 + k, 0:wd], src, ACT.Exp, scale=SCALE_B)\
                       .then_inc(bexp_done, 1)

                def attend(g, j):
                    if j == NT - 1:
                        act.wait_ge(bav_done, count(nxt, AHEAD["bav_done"], 4 * g + 4))
                        copy(ys[:, g, :], ps[:, 4, :]).then_inc(by_ready, 1)

                def join():
                    act.wait_ge(ynT_psum, count(nxt, AHEAD["ynT_psum"], 1))
                    copy(ynT, ps[:, 5, :]).then_inc(ynT_ready, 1)

                def transpose3():
                    act.wait_ge(xh2T_psum, count(nxt, AHEAD["xh2T_psum"], 1))
                    activation(h2T[:, :], ps[:, 5, :], ACT.Identity, bias=ln1[:, 3:4], scale=ln1[:, 2:3])\
                       .then_inc(h2T_ready, 1)

                def transpose2():
                    act.wait_ge(xn2T_psum, count(prv, BEHIND["xn2T_psum"], 1))
                    copy(xn2T[:, :], ps[:, 7, :]).then_inc(xn2T_ready, 1)

                def keys1():
                    act.wait_ge(kqv1_psum, count(prv, BEHIND["kqv1_psum"], 1))
                    activation(k1T, ps[:, 7, :], ACT.Identity, bias=b1col[:, 1:2]).then_inc(kq1_ready, 1)

                def queries1():
                    act.wait_ge(kqv1_psum, count(prv, BEHIND["kqv1_psum"], 2))
                    activation(q1T[:, :], ps[:, 7, 0:FLASH], ACT.Identity, bias=b1col[:, 0:1]).then_inc(kq1_ready, 1)

                def scores1(p):
                    act.wait_ge(s1_psum, count(prv, BEHIND["s1_psum"], p + 1))
                    copy(ss[:, p, :, :].rearrange("p b k -> p (b k)"), ps[:, 7, :]).then_inc(s1_ready, 1)

                def shift1(k):
                    act.wait_ge(sub1_ready, count(prv, BEHIND["sub1_ready"], k + 1))
                    two = ss[:, 2 * k:2 * k + 2, :, :]
                    activation(two, two, ACT.Exp, scale=SCALE_B).then_inc(p1_ready, 1)
                    if k == 3:
                        act.wait_ge(dm1_ready, count(prv, BEHIND["dm1_ready"], 1))
                        activation(dm[:, :, 1:NFB], dm[:, :, 1:NFB], ACT.Exp, scale=SCALE_B).then_inc(fac1_ready, 1)

                def probs_T1(half, kt):
                    act.wait_ge(pT1_psum, count(prv, BEHIND["pT1_psum"], 4 * half + kt + 1))
                    copy(pT[:, kt, :], ps[:, 7, :]).then_inc(pT1_ready, 1)

                def transpose_xq():
                    act.wait_ge(xqT_psum, count(prv, BEHIND["xqT_psum"], 1))
                    copy(xqT, ps[:, 7, :]).then_inc(xqT_ready, 1)

                def gate1(t):
                    act.wait_ge(gate1_psum, count(prv, BEHIND["gate1_psum"], t + 1))
                    if t:
                        act.wait_ge(hq_ready, count(prv, BEHIND["hq_ready"], t))
                    copy(hf[:, :], ps[:, 7, 0:INNER]).then_inc(sgf_done, 1)
                    activation(sgf[:, :], ps[:, 7, 0:INNER], ACT.Tanh, scale=0.5).then_inc(sgf_done, 1)

                def transpose_hq(t):
                    act.wait_ge(hqT_psum, count(prv, BEHIND["hqT_psum"], t + 1))
                    copy(hqT[:, t, :], ps[:, 7, 0:3 * P]).then_inc(hqT_ready, 1)

                def down1():
                    act.wait_ge(out_ready, count(prv, BEHIND["out_ready"], 1))
                    act.dma_start(out[bass.ds(prv[0] + prv[1], 1), :, :].rearrange("a (t p) c -> p (a t) c", p=P),
                                         yout[:, :, :]).then_inc(out_stored, 16)

                steps = dict(load_x=load_x, transpose0=transpose0, transpose1=transpose1, project_v=project_v,
                             exps=exps, attend=attend, join=join, transpose3=transpose3, transpose2=transpose2,
                             keys1=keys1, queries1=queries1, scores1=scores1, shift1=shift1, probs_T1=probs_T1,
                             transpose_xq=transpose_xq, gate1=gate1, transpose_hq=transpose_hq, down1=down1)
                walk(steps, dense, i, nxt, prv)

            pipeline(act, run)

        @block.vector
        def _(dve):
            count = counter(dve, "dve_wait")
            v = nc.vector
            flat = lambda a: a[:, :, :].rearrange("p t c -> p (t c)")

            def norm_stats(src, scratch, link):
                st, mv, ve, ri, ry, rt = scratch
                for t in range(NT):
                    link(v.bn_stats(st[:, t, :], src[:, t, :]), t == NT - 1)
                link(v.tensor_tensor(mv[:, 0, :], st[:, :, 1], st[:, :, 4], ALU.add), False)
                link(v.tensor_tensor(mv[:, 1, :], st[:, :, 1], st[:, :, 4], ALU.subtract), False)
                link(v.tensor_tensor(mv[:, 2, :], st[:, :, 2], st[:, :, 5], ALU.add))
                link(v.tensor_scalar(mv[:, 0, :], mv[:, 0, :], 0.5, None, ALU.mult), False)
                link(v.scalar_tensor_tensor(out=mv[:, 1, :], in0=mv[:, 1, :], scalar=0.25, in1=mv[:, 1, :],
                                            op0=ALU.mult, op1=ALU.mult))
                link(v.scalar_tensor_tensor(out=ve[:, :], in0=mv[:, 2, :], scalar=1.0 / C, in1=mv[:, 1, :],
                                            op0=ALU.mult, op1=ALU.add))
                link(v.tensor_scalar(ve[:, :], ve[:, :], EPS, None, ALU.add))

            def norm_root(scratch, link):
                st, mv, ve, ri, ry, rt = scratch
                link(v.tensor_scalar(ri[:, :], ve[:, :].bitcast(I32), 1, None, ALU.logical_shift_right))
                link(v.tensor_scalar(ry[:, :].bitcast(I32), ri[:, :], -1.0, float(0x5f3759df), ALU.mult, ALU.add))
                for _ in range(3):
                    link(v.scalar_tensor_tensor(out=rt[:, :], in0=ry[:, :], scalar=-0.5, in1=ry[:, :],
                                                op0=ALU.mult, op1=ALU.mult))
                    link(v.tensor_tensor(rt[:, :], rt[:, :], ve[:, :], ALU.mult))
                    link(v.scalar_tensor_tensor(out=ry[:, :], in0=rt[:, :], scalar=1.5, in1=ry[:, :],
                                                op0=ALU.add, op1=ALU.mult))

            def norm_apply(src, dst, scratch, finish):
                st, mv, ve, ri, ry, rt = scratch
                for t in range(NT):
                    finish(v.tensor_scalar(dst[:, t, :], src[:, t, :], mv[:, 0, t:t + 1], ry[:, t:t + 1],
                                           ALU.subtract, ALU.mult))

            def fp4(part_no, src, dst, n, scratch, link, finish):
                a, s, u, x2 = (b[:, 0:n, :] for b in scratch)
                m, r = qm[:, 0:n], qr[:, 0:n]
                over = lambda z: z.unsqueeze(2).to_broadcast([P, n, QBLOCK])
                if part_no == 0:
                    link(v.scalar_tensor_tensor(out=a, in0=src, scalar=-1.0, in1=src, op0=ALU.mult, op1=ALU.max))
                    link(v.tensor_reduce(m, a, AX.X, ALU.max))
                    link(v.tensor_scalar(m, m, 1.0 / FP4_MAX, 1e-12, ALU.mult, ALU.max))
                    link(v.reciprocal(r, m))
                if part_no == 1:
                    link(v.tensor_tensor(a, a, over(r), ALU.mult))
                    link(v.tensor_scalar(s, a, 0.25, None, ALU.is_gt), False)
                    link(v.tensor_scalar(u, a, 2.5, None, ALU.is_gt), False)
                    link(v.tensor_scalar(x2, a, 5.0, 2.0, ALU.is_gt, ALU.mult))
                if part_no == 2:
                    link(v.scalar_tensor_tensor(out=u, in0=a, scalar=3.5, in1=u, op0=ALU.is_gt, op1=ALU.add), False)
                    link(v.scalar_tensor_tensor(out=s, in0=a, scalar=0.75, in1=s, op0=ALU.is_gt, op1=ALU.add))
                    link(v.tensor_tensor(u, u, x2, ALU.add), False)
                if part_no == 3:
                    link(v.scalar_tensor_tensor(out=s, in0=a, scalar=1.25, in1=s, op0=ALU.is_gt, op1=ALU.add))
                    link(v.scalar_tensor_tensor(out=s, in0=a, scalar=1.75, in1=s, op0=ALU.is_gt, op1=ALU.add))
                    link(v.scalar_tensor_tensor(out=s, in0=u, scalar=2.0, in1=s, op0=ALU.mult, op1=ALU.add))
                if part_no == 4:
                    link(v.scalar_tensor_tensor(out=u, in0=s, scalar=0.5, in1=over(m), op0=ALU.mult, op1=ALU.mult))
                    finish(v.scalar_tensor_tensor(out=dst.bitcast(I32), in0=src.bitcast(I32), scalar=-2 ** 31,
                                                  in1=u.bitcast(I32), op0=ALU.bitwise_and, op1=ALU.bitwise_or))

            link_no = [0]

            def link0(ins, settle=True):
                link_no[0] += 1
                ins.then_inc(prep_dve, 1)
                if settle:
                    dve.wait_ge(prep_dve, link_no[0])

            link0(v.memset(wguR, 0.0), False)
            link0(v.memset(wdR, 0.0), False)
            link0(v.memset(ones, 1.0), False)
            link0(v.memset(vones[:, :], 1.0), False)
            link0(v.memset(hpad[:, 0:2], 0.0), False)
            link0(v.memset(nmx[:, :, :], 0.0), False)
            link0(v.memset(kst[:, :, :].bitcast(I32), 0), False)
            link0(v.memset(qst[:, :, :].bitcast(I32), 0))
            link0(v.memset(kst[SHIFT_ROW:P, :, :], 1.0))
            dve.wait_ge(weights_loaded, 16 * PREP_LOADS)
            link0(v.tensor_copy(ident_b[:, :], ident[:, :]), False)
            link0(v.tensor_copy(up_b[:, :], masks[:, 0:P]), False)
            link0(v.tensor_copy(low_b[:, :], masks[:, P:2 * P]), False)
            link0(v.tensor_copy(m1_b[:, :], masks[:, 2 * P:2 * P + FLASH]), False)
            hd = DB // 2
            for z in range(2):
                src = wqkraw[:, z * C:(z + 1) * C].rearrange("c (h d) -> c d h", d=DB)
                link0(v.tensor_copy(wrot[:, 2 * z, :, :], src), False)
                link0(v.tensor_copy(wrot[:, 2 * z + 1, 0:hd, :], src[:, hd:DB, :]), False)
                link0(v.tensor_copy(wrot[:, 2 * z + 1, hd:DB, :], src[:, 0:hd, :]))
            wq = [view(share_s, [P, 48, QBLOCK], 768 * k) for k in range(4)]
            for g, n in ((wguR.rearrange("p a (b k) -> p (a b) k", k=QBLOCK), 6 * C // QBLOCK),
                         (wdR.rearrange("p (b k) -> p b k", k=QBLOCK), INNER_PAD // QBLOCK)):
                for k in range(5):
                    fp4(k, g, g, n, wq, link0, link0)
            dve.wait_ge(prep_pe, PREP_PE)
            link0(v.tensor_copy(wdT[:, :, :].rearrange("p a c -> p (a c)"), ps[:, 4, 0:3 * C]))
            assert link_no[0] == PREP_DVE, (link_no[0], "PREP_DVE")
            prep_over(dve)

            def run(i, nxt, prv):
                a_steps, b_steps = [0], [0]

                def settle_a():
                    dve.wait_ge(ahead_step, count(nxt, AHEAD_STEPS, a_steps[0]))

                def settle_b():
                    dve.wait_ge(behind_step, count(prv, BEHIND_STEPS, b_steps[0]))

                def link_a(ins, now=True):
                    a_steps[0] += 1
                    ins.then_inc(ahead_step, 1)
                    if now:
                        settle_a()

                def link_b(ins, now=True):
                    b_steps[0] += 1
                    ins.then_inc(behind_step, 1)
                    if now:
                        settle_b()

                def row_sums(h):
                    dve.wait_ge(aexp_done, count(i, DENSE["aexp_done"], 4 * h + 4))
                    v.reciprocal(rla[:, h, :], la[:, h, :]).then_inc(rl_ready, 1)

                def expert_y(n):
                    e, c = n // CHUNKS, n % CHUNKS
                    dve.wait_ge(silu_done, count(i, DENSE["silu_done"], n + 1))
                    if n == 0:
                        dve.wait_ge(zav_done, count(i, DENSE["zav_done"], PAIRS))
                    if e >= 2 and c == 0:
                        dve.wait_ge(down_psum, count(i, DENSE["down_psum"], NT * (e - 1)))
                    v.scalar_tensor_tensor(out=sg[:, n % 2, :], in0=sg[:, n % 2, :], scalar=1.0,
                                                in1=ps[:, (2 * n) % 3, :], op0=ALU.add, op1=ALU.mult)\
                                                   .then_inc(gate_read, 1)
                    dve.wait_ge(value_psum, count(i, DENSE["value_psum"], n + 1))
                    dve.wait_ge(gate_read, count(i, DENSE["gate_read"], n + 1))
                    v.scalar_tensor_tensor(out=ym[:, e % 2, c, :], in0=sg[:, n % 2, :], scalar=0.5,
                                                in1=ps[:, (2 * n + 1) % 3, :], op0=ALU.mult, op1=ALU.mult)\
                                                   .then_inc(moe_y, 1)

                def expert_acc(e):
                    dve.wait_ge(down_psum, count(i, DENSE["down_psum"], NT * (e + 1)))
                    if e:
                        dve.wait_ge(moe_acc, count(i, DENSE["moe_acc"], e))
                    else:
                        dve.wait_ge(ao_added, count(i, DENSE["ao_added"], 1))
                    for t in range(NT):
                        ins = v.scalar_tensor_tensor(out=xacc[:, t, :], in0=ps[:, 3, t * P:(t + 1) * P],
                                                     scalar=hotd[:, t, e:e + 1], in1=xacc[:, t, :],
                                                     op0=ALU.mult, op1=ALU.add)
                    ins.then_inc(moe_acc, 1)

                def dense(pos):
                    h, t = pos // 4, pos % 4
                    if pos == 0:
                        dve.wait_ge(hot_ready, count(i, AHEAD["hot_ready"], 1))
                        v.tensor_copy(hotd[:, :, :], hot[:, :, :])
                        v.tensor_copy(xacc[:, :, :], xin[:, :, :]).then_inc(carried, 1)
                    if h < HEADS:
                        dve.wait_ge(as_psum, count(i, DENSE["as_psum"], pos + 1))
                        v.tensor_reduce(nma[:, h, t:t + 1], ps[:, pos % 3, 0:P * (t + 1)], AX.X, ALU.max,
                                             negate=True).then_inc(amax, 1)
                        if h and t == 1:
                            row_sums(h - 1)
                        return
                    n = h - HEADS
                    if n == 0 and t == 0:
                        row_sums(HEADS - 1)
                    if n == 1 and t == 3:
                        dve.wait_ge(ao_psum, count(i, DENSE["ao_psum"], 1))
                        dve.wait_ge(carried, count(i, DENSE["carried"], 1))
                        v.tensor_tensor(flat(xacc), flat(xacc), ps[:, 3, :], ALU.add).then_inc(ao_added, 1)
                    if t == 2:
                        expert_y(n)
                    if n >= 6 and n % 4 == 2 and t == 3:
                        expert_acc(n // 4 - 1)
                    if n == 15 and t == 3:
                        expert_acc(EXPERTS - 1)

                def ln0_stats():
                    dve.wait_ge(x_loaded, count(nxt, AHEAD["x_loaded"], 16))
                    norm_stats(xin, norm_scratch[0], link_a)

                def ln0_apply():
                    norm_apply(xin, xn, norm_scratch[0], lambda ins: ins.then_inc(xn_ready, 1))

                def ln1_stats():
                    dve.wait_ge(xn_ready, count(nxt, AHEAD["xn_ready"], 4))
                    norm_stats(xn, norm_scratch[0], link_a)

                def ln1_apply():
                    norm_apply(xn, xh, norm_scratch[0], lambda ins: ins.then_inc(xh_ready, 1))

                def conv():
                    dve.wait_ge(h_ready, count(nxt, AHEAD["h_ready"], 1))
                    link_a(v.tensor_scalar(hc, hpad[:, 2:T + 2], convw[:, 2:3], None, ALU.mult))
                    link_a(v.scalar_tensor_tensor(out=hc, in0=hpad[:, 1:T + 1], scalar=convw[:, 1:2],
                                                  in1=hc, op0=ALU.mult, op1=ALU.add))
                    v.scalar_tensor_tensor(out=hc, in0=hpad[:, 0:T], scalar=convw[:, 0:1],
                                                in1=hc, op0=ALU.mult, op1=ALU.add).then_inc(conv_ready, 1)

                def rotate(z):
                    dve.wait_ge(qk_psum, count(nxt, AHEAD["qk_psum"], 2 * z + 2))
                    if z:
                        dve.wait_ge(split_ready, count(nxt, AHEAD["split_ready"], 3))
                    link_a(v.tensor_tensor(rope[:, 0, :], ps[:, 5, :], cosT, ALU.mult), False)
                    v.tensor_tensor(rope[:, 1, :], ps[:, 6, :], sinT, ALU.mult).then_inc(rope_read, 1)
                    dve.wait_ge(rope_read, count(nxt, AHEAD["rope_read"], z + 1))
                    link_a(v.tensor_tensor(rope[:, 0, :], rope[:, 0, :], rope[:, 1, :], ALU.add))

                def split(z):
                    f, r = rope[:, 0, :], rope[:, 1, :]
                    v.tensor_copy(part[:, z, 0, :], f).then_inc(split_ready, 1)
                    dve.wait_ge(split_ready, count(nxt, AHEAD["split_ready"], 3 * z + 1))
                    link_a(v.tensor_tensor(r, f, part[:, z, 0, :], ALU.subtract))
                    v.tensor_copy(part[:, z, 1, :], r).then_inc(split_ready, 1)
                    dve.wait_ge(split_ready, count(nxt, AHEAD["split_ready"], 3 * z + 2))
                    v.tensor_tensor(part[:, z, 2, :], r, part[:, z, 1, :], ALU.subtract).then_inc(split_ready, 1)

                def row_max(u):
                    t, h, k = MAX_UNITS[u]
                    wd = P * (t + 1)
                    dve.wait_ge(bs_psum, count(nxt, AHEAD["bs_psum"], u + 1))
                    src = ps[:, 5 + u % 2, 0:k * wd].rearrange("p (k w) -> p k w", w=wd)
                    v.tensor_reduce(nmx[:, h:h + k, t], src, AX.X, ALU.max, negate=True).then_inc(bmax_ready, 1)

                def shift_rows():
                    dve.wait_ge(mxT_psum, count(nxt, AHEAD["mxT_psum"], 1))
                    src = ps[0:HEADS * NT, 5, 0:P]
                    v.tensor_copy(mx3[:, 0, :], src).then_inc(mx_split, 1)
                    dve.wait_ge(mx_split, count(nxt, AHEAD["mx_split"], 1))
                    link_a(v.tensor_tensor(mxr[:, :], src, mx3[:, 0, :], ALU.subtract))
                    v.tensor_copy(mx3[:, 1, :], mxr[:, :]).then_inc(mx_split, 1)
                    dve.wait_ge(mx_split, count(nxt, AHEAD["mx_split"], 2))
                    v.tensor_tensor(mx3[:, 2, :], mxr[:, :], mx3[:, 1, :], ALU.subtract).then_inc(mx_split, 1)

                def divide(t):
                    dve.wait_ge(byT_psum, count(nxt, AHEAD["byT_psum"], t + 1))
                    y4 = ps[:, 5 + t % 2, :].rearrange("p (h d) -> p h d", d=32)
                    link_a(v.reciprocal(rb[:, t, :], y4[:, :, DB]))
                    v.tensor_tensor(yn[:, t, :].rearrange("p (h d) -> p h d", d=DB), y4[:, :, 0:DB],
                                         rb[:, t, :].unsqueeze(2).to_broadcast([P, HEADS, DB]), ALU.mult)\
                                            .then_inc(yn_ready, 1)

                def project_y():
                    dve.wait_ge(bo_psum, count(nxt, AHEAD["bo_psum"], 1))
                    v.tensor_tensor(flat(x1), flat(xn), ps[:, 6, :], ALU.add).then_inc(x1_ready, 1)

                def ln3_stats():
                    dve.wait_ge(x1_ready, count(nxt, AHEAD["x1_ready"], 1))
                    norm_stats(x1, norm_scratch[0], link_a)

                def ln3_apply():
                    norm_apply(x1, xh, norm_scratch[0], lambda ins: ins.then_inc(xh2_ready, 1))
                    link_a(v.tensor_tensor(flat(xin), flat(xin), flat(x1), ALU.add), False)

                def route():
                    dve.wait_ge(logits_psum, count(nxt, AHEAD["logits_psum"], 1))
                    if i is not None:
                        dve.wait_ge(carried, count(i, DENSE["carried"], 1))
                    link_a(v.tensor_copy(flat(lg), ps[:, 6, 0:NT * EXPERTS]))
                    link_a(v.tensor_reduce(lmax[:, :], lg[:, :, :], AX.X, ALU.max))
                    link_a(v.tensor_tensor(lg[:, :, :], lg[:, :, :],
                                           lmax[:, :].unsqueeze(2).to_broadcast([P, NT, EXPERTS]), ALU.is_equal))
                    link_a(v.tensor_copy(hot[:, :, 0], lg[:, :, 0]), False)
                    link_a(v.tensor_copy(taken[:, :], lg[:, :, 0]))
                    for e in range(1, EXPERTS):
                        ins = v.tensor_tensor(hot[:, :, e], lg[:, :, e], taken[:, :], ALU.is_gt)
                        if e == EXPERTS - 1:
                            ins.then_inc(hot_ready, 1)
                        else:
                            link_a(ins)
                            link_a(v.tensor_tensor(taken[:, :], taken[:, :], lg[:, :, e], ALU.max))

                def take_over():
                    dve.wait_ge(moe_acc, count(prv, DENSE["moe_acc"], EXPERTS))
                    link_b(v.tensor_copy(xp[:, :, :], xacc[:, :, :]))

                def values1():
                    dve.wait_ge(kqv1_psum, count(prv, BEHIND["kqv1_psum"], 3))
                    v.tensor_tensor(v1, ps[:, 7, :].rearrange("p (t c) -> p t c", c=C),
                                         b1bc[:, 0, :].unsqueeze(1).to_broadcast([P, NT, C]), ALU.add)\
                                            .then_inc(v1_ready, 1)

                wide = lambda a: a.rearrange("p a b -> p (a b)")

                def block_max1(half):
                    dve.wait_ge(s1_ready, count(prv, BEHIND["s1_ready"], 4 * half + 4))
                    link_b(v.tensor_reduce(bm[:, 4 * half:4 * half + 4, :], ss[:, 4 * half:4 * half + 4, :, :],
                                           AX.X, ALU.max))

                def running_max1():
                    for near, (src, dst) in ((1, (bm, rm)), (2, (rm, bm)), (4, (bm, rm))):
                        link_b(v.tensor_copy(dst[:, :, 0:near], src[:, :, 0:near]), False)
                        link_b(v.tensor_tensor(dst[:, :, near:NFB], src[:, :, near:NFB], src[:, :, 0:NFB - near],
                                               ALU.max))

                def shift1(k):
                    two = ss[:, 2 * k:2 * k + 2, :, :].rearrange("p a b k -> p (a b) k")
                    v.tensor_tensor(two, two, wide(rm[:, 2 * k:2 * k + 2, :]).unsqueeze(2).to_broadcast(
                        [P, 2 * NFB, FLASH]), ALU.subtract).then_inc(sub1_ready, 1)
                    if k == 3:
                        v.tensor_tensor(dm[:, :, 1:NFB], rm[:, :, 0:NFB - 1], rm[:, :, 1:NFB], ALU.subtract)\
                           .then_inc(dm1_ready, 1)

                def sum1(k):
                    dve.wait_ge(p1_ready, count(prv, BEHIND["p1_ready"], k + 1))
                    v.tensor_reduce(ll[:, 2 * k:2 * k + 2, :], ss[:, 2 * k:2 * k + 2, :, :], AX.X, ALU.add)\
                       .then_inc(sum1_ready, 1)

                def ratios1():
                    dve.wait_ge(totals_ready, count(prv, BEHIND["totals_ready"], 1))
                    link_b(v.reciprocal(rl[:, :, :], ll[:, :, :]))
                    link_b(v.tensor_tensor(rr[:, :, 1:NFB], ll[:, :, 0:NFB - 1], rl[:, :, 1:NFB], ALU.mult), False)
                    link_b(v.memset(rr[:, :, 0:1], 0.0), False)
                    link_b(v.tensor_copy(cc[:, :], rl[:, :, NFB - 1]))
                    v.tensor_scalar(dm[:, :, :], rr[:, :, :], -1.0, 1.0, ALU.mult, ALU.add).then_inc(ratios_ready, 1)

                def mix1(half):
                    dve.wait_ge(o1_psum, count(prv, BEHIND["o1_psum"], half + 1))
                    v.tensor_tensor(om[:, 8 * half:8 * half + 8, :],
                                         ps[:, 7, :].rearrange("p (h q) -> p h q", q=FLASH),
                                         blk[:, 8 * half:8 * half + 8].unsqueeze(2).to_broadcast([C, 8, FLASH]),
                                         ALU.mult).then_inc(om_ready, 1)

                def project1():
                    dve.wait_ge(om_ready, count(prv, BEHIND["om_ready"], 2))
                    v.tensor_reduce(oT[:, :], om.rearrange("p h q -> p q h"), AX.X, ALU.add).then_inc(oT1_ready, 1)
                    link_b(v.tensor_tensor(xp[:, :, :], xp[:, :, :],
                                           b1bc[:, 1, :].unsqueeze(1).to_broadcast([P, NT, C]), ALU.add))

                blocks = lambda a: a.rearrange("p t (b k) -> p (t b) k", k=QBLOCK)

                def round_x(k):
                    if k == 1:
                        dve.wait_ge(pr1_psum, count(prv, BEHIND["pr1_psum"], 1))
                        v.tensor_tensor(xp[P - FLASH:P, NT - 1, :], xp[P - FLASH:P, NT - 1, :],
                                             ps[P - FLASH:P, 7, 0:C], ALU.add).then_inc(pr1_added, 1)
                    fp4(k, blocks(xn2[:, :, :]), blocks(xq), NQ, (qa, qc, qd, qe), link_b,
                        lambda ins: ins.then_inc(xq_ready, 1))

                def up1(t):
                    dve.wait_ge(up1_psum, count(prv, BEHIND["up1_psum"], t + 1))
                    dve.wait_ge(sgf_done, count(prv, BEHIND["sgf_done"], 2 * t + 2))
                    link_b(v.scalar_tensor_tensor(out=sgf, in0=sgf, scalar=1.0, in1=hf, op0=ALU.add, op1=ALU.mult))
                    v.scalar_tensor_tensor(out=hf, in0=sgf, scalar=0.5, in1=ps[:, 7, 0:INNER], op0=ALU.mult,
                                                op1=ALU.mult).then_inc(hf_done, 1)

                def round_h(t, k):
                    if k == 0:
                        dve.wait_ge(hf_done, count(prv, BEHIND["hf_done"], t + 1))
                        if t:
                            dve.wait_ge(hq_ready, count(prv, BEHIND["hq_ready"], t))
                        else:
                            dve.wait_ge(xq_ready, count(prv, BEHIND["xq_ready"], 1))
                        if t == 0:
                            link_b(v.memset(hq[:, :, INNER:INNER_PAD], 0.0), False)
                    if k == 4 and t >= 2:
                        dve.wait_ge(hqT_psum, count(prv, BEHIND["hqT_psum"], t - 1))
                    cut = lambda a: a.rearrange("p (b k) -> p b k", k=QBLOCK)
                    fp4(k, cut(hf), cut(hq[:, t % 2, 0:INNER]), INNER // QBLOCK, (qa, qc, qd, qe), link_b,
                        lambda ins: ins.then_inc(hq_ready, 1))

                def down1():
                    dve.wait_ge(pr1_added, count(prv, BEHIND["pr1_added"], 1))
                    dve.wait_ge(dn_psum, count(prv, BEHIND["dn_psum"], 1))
                    v.tensor_tensor(flat(yout), flat(xp), ps[:, 7, :], ALU.add).then_inc(out_ready, 1)

                steps = dict(
                    ln0_stats=ln0_stats, ln0_root=lambda: norm_root(norm_scratch[0], link_a), ln0_apply=ln0_apply,
                    ln1_stats=ln1_stats, ln1_root=lambda: norm_root(norm_scratch[0], link_a), ln1_apply=ln1_apply,
                    conv=conv, project_q=lambda: rotate(0), split_q=lambda: split(0), project_k=lambda: rotate(1),
                    split_k=lambda: split(1), row_max=row_max, shift_rows=shift_rows, divide=divide,
                    project_y=project_y, ln3_stats=ln3_stats,
                    ln3_root=lambda: norm_root(norm_scratch[0], link_a), ln3_apply=ln3_apply, route=route,
                    ln2_stats=lambda: norm_stats(xp, norm_scratch[1], link_b),
                    ln2_root=lambda: norm_root(norm_scratch[1], link_b),
                    ln2_apply=lambda: norm_apply(xp, xn2, norm_scratch[1], lambda ins: ins.then_inc(xn2_ready, 1)),
                    values1=values1, block_max1=block_max1, running_max1=running_max1,
                    shift1=shift1, sum1=sum1,
                    ratios1=ratios1, mix1=mix1, project1=project1, round_x=round_x,
                    up1=up1, round_h=round_h, down1=down1)
                if prv is not None:
                    take_over()
                walk(steps, dense, i, nxt, prv)
                if prv is not None:
                    dve.wait_ge(out_stored, count(prv, BEHIND["out_stored"], 16))
                if nxt is not None:
                    assert a_steps[0] == AHEAD_STEPS, (a_steps[0], "AHEAD_STEPS")
                if prv is not None:
                    assert b_steps[0] == BEHIND_STEPS, (b_steps[0], "BEHIND_STEPS")

            pipeline(dve, run)

        @block.tensor
        def _(pe):
            count = counter(pe, "pe_wait")
            mm, tr = nc.tensor.matmul, nc.tensor.transpose
            idn = ident[:, :]

            pe.wait_ge(weights_loaded, 16 * PREP_LOADS)
            pe.wait_ge(prep_dve, 3)
            for g in range(4):
                for h in range(4 * g, 4 * g + 4):
                    ins = mm(ps[:, g, (h % 4) * C:(h % 4 + 1) * C], wkq[:, 1, h, :], wkq[:, 0, h, :],
                             start=True, stop=True)
                ins.then_inc(prep_pe, 1)
            for g in range(2):
                for k in range(4):
                    ins = tr(ps[:, 4 + g, k * C:(k + 1) * C], raw[:, 4 * g + k, :], idn)
                ins.then_inc(prep_pe, 1)
            for g in range(2):
                for k in range(4):
                    n = 4 * g + k
                    ins = tr(ps[:, 6 + g, k * C:(k + 1) * C], raw2[:, n * C:(n + 1) * C], idn)
                ins.then_inc(prep_pe, 1)
            pe.wait_ge(prep_act, 1)
            for k in range(4):
                ins = tr(ps[:, 0, k * C:(k + 1) * C], w1raw[:, k, :], idn)
            ins.then_inc(prep_pe, 1)
            pe.wait_ge(prep_act, 2)
            mm(ps[:, 1, 0:2 * C], ones, brow, start=True, stop=True).then_inc(prep_pe, 1)
            pe.wait_ge(prep_act, 5)
            pe.wait_ge(prep_dve, PREP_DVE - 1)
            for k in range(6):
                ins = tr(ps[:, 2 + k // 3, (k % 3) * C:(k % 3 + 1) * C], wguR[:, k, :], idn)
                if k % 3 == 2:
                    ins.then_inc(prep_pe, 1)
            for k in range(3):
                tr(ps[:, 4, k * C:(k + 1) * C], wdR[:, k * C:(k + 1) * C], idn).then_inc(prep_pe, 1)
            prep_over(pe)

            tile = lambda t: slice(t * P, (t + 1) * P)

            def transpose_tiles(src, bank):
                for t in range(NT):
                    ins = tr(ps[:, bank, tile(t)], src[:, t, :], idn)
                return ins

            def run(i, nxt, prv):
                def value_side(p):
                    if p:
                        pe.wait_ge(g_ready, count(i, DENSE["g_ready"], 2 * p))
                    elif prv is not None:
                        pe.wait_ge(moe_acc, count(prv, DENSE["moe_acc"], EXPERTS))
                    for t in range(NT):
                        ins = mm(ps[:, 3, tile(t)], xnTd[:, tile(t)], wvT[:, 2 * DA * p:2 * DA * (p + 1)],
                                 start=True, stop=True)
                    ins.then_inc(avp_psum, 1)

                def key_side(h):
                    if h % 2 == 0:
                        pe.wait_ge(av_ready, count(i, DENSE["av_ready"], h // 2 + 1))
                    else:
                        pe.wait_ge(g_ready, count(i, DENSE["g_ready"], h))
                    mm(ps[:, 3, :], mg[:, h, :], xnTd[:, :], start=True, stop=True).then_inc(g_psum, 1)

                def values(p):
                    pe.wait_ge(vn_ready, count(i, DENSE["vn_ready"], 2 * p + 2))
                    if p:
                        pe.wait_ge(z_ready, count(i, DENSE["z_ready"], p))
                    else:
                        pe.wait_ge(by_ready, count(i, AHEAD["by_ready"], 4))
                    for t in range(NT - 1, -1, -1):
                        for k in range(2):
                            h = 2 * p + k
                            ins = mm(ps[DA * k:DA * k + DA, 4, 0:P * (t + 1)], vn[:, h % 4, t, :],
                                     pa[:, h % 4, OFF[t]:OFF[t] + P * (t + 1)], start=(t == NT - 1), stop=(t == 0))
                    ins.then_inc(zav_done, 1)

                def down(e, t):
                    if t == 0:
                        pe.wait_ge(moe_y, count(i, DENSE["moe_y"], 4 * e + 4))
                        if e:
                            pe.wait_ge(moe_acc, count(i, DENSE["moe_acc"], e))
                        else:
                            pe.wait_ge(ao_added, count(i, DENSE["ao_added"], 1))
                    for c in range(CHUNKS):
                        ins = mm(ps[:, 3, tile(t)], ym[:, e % 2, c, tile(t)], wdn[:, e, c, :],
                                 start=(c == 0), stop=(c == CHUNKS - 1))
                    ins.then_inc(down_psum, 1)

                def dense(pos):
                    h, t = pos // 4, pos % 4
                    if pos == 0:
                        pe.wait_ge(xnTd_ready, count(i, DENSE["xnTd_ready"], 1))
                        value_side(0)
                        key_side(0)
                    if h < HEADS:
                        if t == 0:
                            if h % 2 and h + 1 < HEADS:
                                value_side((h + 1) // 2)
                            pe.wait_ge(g_ready, count(i, DENSE["g_ready"], h + 1))
                        if t == 2 and h + 1 < HEADS:
                            key_side(h + 1)
                        if pos >= 3:
                            pe.wait_ge(aexp_done, count(i, DENSE["aexp_done"], pos - 2))
                        b = pos % 3
                        mm(ps[:, b, 0:P * (t + 1)], xnTd[:, tile(t)], gs[:, h % 2, 0:P * (t + 1)],
                           start=True, stop=False)
                        mm(ps[:, b, tile(t)], ident_b[:, :], up_b[:, :], start=False, stop=True).then_inc(as_psum, 1)
                        if t == 3 and h >= 2 and h % 2 == 0:
                            values(h // 2 - 1)
                        return
                    n = h - HEADS
                    e, c = n // CHUNKS, n % CHUNKS
                    if n == 0 and t == 0:
                        pe.wait_ge(h2Td_ready, count(i, DENSE["h2Td_ready"], 1))
                        pe.wait_ge(aexp_done, count(i, DENSE["aexp_done"], 4 * HEADS))
                    if t == 0:
                        if n >= 2:
                            pe.wait_ge(moe_y, count(i, DENSE["moe_y"], n - 1))
                        mm(ps[:, (2 * n) % 3, :], wgv[:, e, c * P:(c + 1) * P], h2Td[:, :],
                                start=True, stop=True).then_inc(gate_psum, 1)
                        if n == 0:
                            values(PAIRS - 1)
                    if t == 1:
                        if n:
                            pe.wait_ge(gate_read, count(i, DENSE["gate_read"], n))
                        mm(ps[:, (2 * n + 1) % 3, :], wgv[:, e, DFF + c * P:DFF + (c + 1) * P], h2Td[:, :],
                                start=True, stop=True).then_inc(value_psum, 1)
                    if n == 1 and t == 2:
                        pe.wait_ge(z_ready, count(i, DENSE["z_ready"], PAIRS))
                        pe.wait_ge(g_ready, count(i, DENSE["g_ready"], HEADS))
                        for q in range(NT):
                            for p in range(PAIRS):
                                ins = mm(ps[:, 3, tile(q)], zT[:, p, tile(q)], woT[:, p, :],
                                         start=(p == 0), stop=(p == PAIRS - 1))
                        ins.then_inc(ao_psum, 1)
                    if n >= 5 and n % 4 == 1 and t >= 2:
                        for q in (2 * (t - 2), 2 * (t - 2) + 1):
                            down(n // 4 - 1, q)
                    if n == 15 and t == 3:
                        for q in range(NT):
                            down(EXPERTS - 1, q)

                def transpose0():
                    pe.wait_ge(xn_ready, count(nxt, AHEAD["xn_ready"], 4))
                    transpose_tiles(xn, 5).then_inc(xnT_psum, 1)

                def transpose1():
                    pe.wait_ge(xh_ready, count(nxt, AHEAD["xh_ready"], 4))
                    transpose_tiles(xh, 6).then_inc(xhT_psum, 1)

                def project(z):
                    if z == 0:
                        pe.wait_ge(conv_ready, count(nxt, AHEAD["conv_ready"], 1))
                    else:
                        pe.wait_ge(rope_read, count(nxt, AHEAD["rope_read"], 1))
                    for k in range(2):
                        mm(ps[:, 5 + k, :], wrot[:, 2 * z + k, :, :].rearrange("c d h -> c (d h)"), hc,
                                start=True, stop=True).then_inc(qk_psum, 1)

                def project_v():
                    pe.wait_ge(rope_read, count(nxt, AHEAD["rope_read"], 2))
                    for t in range(NT):
                        ins = mm(ps[:, 5, tile(t)], hc[:, tile(t)], wbv[:, :], start=True, stop=True)
                    ins.then_inc(bv_psum, 1)

                def row_max(u):
                    t, h0, k = MAX_UNITS[u]
                    wd, b = P * (t + 1), 5 + u % 2
                    if u == 0:
                        pe.wait_ge(bv_ready, count(nxt, AHEAD["bv_ready"], 1))
                        pe.wait_ge(stack_loaded, count(nxt, AHEAD["stack_loaded"], 16 * 18))
                    if u >= 2:
                        pe.wait_ge(bmax_ready, count(nxt, AHEAD["bmax_ready"], u - 1))
                    for h in range(h0, h0 + k):
                        o = (h - h0) * wd
                        mm(ps[:, b, o:o + wd], qst[0:SHIFT_ROW, h, tile(t)], kst[0:SHIFT_ROW, h, 0:wd],
                           start=True, stop=False)
                        ins = mm(ps[:, b, o + t * P:o + wd], ident_b[:, :], up_b[:, :], start=False, stop=True)
                    ins.then_inc(bs_psum, 1)

                def shift_rows():
                    pe.wait_ge(bmax_ready, count(nxt, AHEAD["bmax_ready"], UNITS))
                    tr(ps[:, 5, 0:P], nmx[:, :, :].rearrange("p h t -> p (h t)"), idn).then_inc(mxT_psum, 1)

                def exps(u):
                    j, h0, k = EXP_UNITS[u]
                    wd, b = T - P * j, 5 + u % 2
                    if u == 0:
                        pe.wait_ge(shift_loaded, count(nxt, AHEAD["shift_loaded"], 48))
                    if u >= 2:
                        pe.wait_ge(bexp_done, count(nxt, AHEAD["bexp_done"], u - 1))
                    for h in range(h0, h0 + k):
                        o = (h - h0) * wd
                        mm(ps[:, b, o:o + wd], kst[0:SHIFT_ROW + PARTS, h, tile(j)],
                           qst[0:SHIFT_ROW + PARTS, h, j * P:T], start=True, stop=False)
                        ins = mm(ps[:, b, o:o + P], ident_b[:, :], low_b[:, :], start=False, stop=True)
                    ins.then_inc(bst_psum, 1)

                def attend(g, j):
                    n = 4 * g + j
                    pe.wait_ge(bexp_done, count(nxt, AHEAD["bexp_done"], EXP_END[g, j]))
                    if j == 0:
                        if g:
                            pe.wait_ge(by_ready, count(nxt, AHEAD["by_ready"], g))
                        elif i is not None:
                            pe.wait_ge(z_ready, count(i, DENSE["z_ready"], PAIRS))
                    for k in range(4):
                        c0 = (j * HEADS + 4 * g + k) * VCOLS
                        ins = mm(ps[32 * k:32 * k + 32, 4, j * P:T], vones[:, c0:c0 + 32],
                                 pt[:, n % 2, k, 0:T - j * P], start=(j == 0), stop=(j == NT - 1))
                    ins.then_inc(bav_done, 1)

                def divide(t):
                    if t == 0:
                        pe.wait_ge(by_ready, count(nxt, AHEAD["by_ready"], 4))
                    if t >= 2:
                        pe.wait_ge(yn_ready, count(nxt, AHEAD["yn_ready"], t - 1))
                    for g in range(4):
                        ins = tr(ps[:, 5 + t % 2, tile(g)], ys[:, g, tile(t)], idn)
                    ins.then_inc(byT_psum, 1)

                def join():
                    pe.wait_ge(yn_ready, count(nxt, AHEAD["yn_ready"], 4))
                    transpose_tiles(yn, 5).then_inc(ynT_psum, 1)

                def project_y():
                    pe.wait_ge(ynT_ready, count(nxt, AHEAD["ynT_ready"], 1))
                    for t in range(NT):
                        ins = mm(ps[:, 6, tile(t)], ynT[:, tile(t)], wproj[:, :], start=True, stop=True)
                    ins.then_inc(bo_psum, 1)

                def transpose3():
                    pe.wait_ge(xh2_ready, count(nxt, AHEAD["xh2_ready"], 4))
                    transpose_tiles(xh, 5).then_inc(xh2T_psum, 1)

                def route():
                    pe.wait_ge(h2T_ready, count(nxt, AHEAD["h2T_ready"], 1))
                    for t in range(NT):
                        ins = mm(ps[:, 6, t * EXPERTS:(t + 1) * EXPERTS], h2T[:, tile(t)], wrt[:, :],
                                 start=True, stop=True)
                    ins.then_inc(logits_psum, 1)

                def transpose2():
                    pe.wait_ge(xn2_ready, count(prv, BEHIND["xn2_ready"], 4))
                    transpose_tiles(xn2, 7).then_inc(xn2T_psum, 1)

                def keys1():
                    pe.wait_ge(xn2T_ready, count(prv, BEHIND["xn2T_ready"], 1))
                    mm(ps[:, 7, :], w1T[:, 1, :], xn2T[:, :], start=True, stop=True).then_inc(kqv1_psum, 1)

                def queries1():
                    pe.wait_ge(kq1_ready, count(prv, BEHIND["kq1_ready"], 1))
                    mm(ps[:, 7, 0:FLASH], w1T[:, 0, :], xn2T[:, T - FLASH:T], start=True, stop=True)\
                       .then_inc(kqv1_psum, 1)

                def values1():
                    pe.wait_ge(kq1_ready, count(prv, BEHIND["kq1_ready"], 2))
                    for t in range(NT):
                        ins = mm(ps[:, 7, tile(t)], xn2T[:, tile(t)], w1T[:, 2, :], start=True, stop=True)
                    ins.then_inc(kqv1_psum, 1)

                def scores1(p):
                    if p == 0:
                        pe.wait_ge(v1_ready, count(prv, BEHIND["v1_ready"], 1))
                        pe.wait_ge(qbd_ready, count(prv, BEHIND["qbd_ready"], 1))
                    else:
                        pe.wait_ge(s1_ready, count(prv, BEHIND["s1_ready"], p))
                    mm(ps[:, 7, :], qbd[:, 2 * p:2 * p + 2, :].rearrange("c h q -> c (h q)"), k1T,
                       start=True, stop=False)
                    mm(ps[:, 7, T - FLASH:T], ident_b[:, :], m1_b[:, :], start=False, stop=True).then_inc(s1_psum, 1)

                def probs_T1(half, kt):
                    r = 4 * half + kt
                    if kt == 0:
                        pe.wait_ge(pw1_ready, count(prv, BEHIND["pw1_ready"], 2 * half + 2))
                        if half:
                            pe.wait_ge(om_ready, count(prv, BEHIND["om_ready"], 1))
                        else:
                            pe.wait_ge(s1_ready, count(prv, BEHIND["s1_ready"], PAIRS))
                    else:
                        pe.wait_ge(pT1_ready, count(prv, BEHIND["pT1_ready"], r))
                    for k in range(4):
                        src = ss[:, 4 * half + k, 2 * kt:2 * kt + 2, :].rearrange("p b k -> p (b k)")
                        ins = tr(ps[:, 7, tile(k)], src, idn)
                    ins.then_inc(pT1_psum, 1)

                def mix1(half):
                    pe.wait_ge(pT1_ready, count(prv, BEHIND["pT1_ready"], 4 * half + 4))
                    for kt in range(NT):
                        ins = mm(ps[:, 7, :], v1[:, kt, :], pT[:, kt, :], start=(kt == 0), stop=(kt == NT - 1))
                    ins.then_inc(o1_psum, 1)

                def project1():
                    pe.wait_ge(oT1_ready, count(prv, BEHIND["oT1_ready"], 1))
                    mm(ps[P - FLASH:P, 7, 0:C], oT[:, :], w1T[:, 3, :], start=True, stop=True).then_inc(pr1_psum, 1)

                def transpose_xq():
                    pe.wait_ge(pr1_added, count(prv, BEHIND["pr1_added"], 1))
                    pe.wait_ge(xq_ready, count(prv, BEHIND["xq_ready"], 1))
                    transpose_tiles(xq, 7).then_inc(xqT_psum, 1)

                def gate1(t):
                    if t:
                        pe.wait_ge(hqT_ready, count(prv, BEHIND["hqT_ready"], t))
                    else:
                        pe.wait_ge(xqT_ready, count(prv, BEHIND["xqT_ready"], 1))
                    mm(ps[:, 7, 0:INNER], xqT[:, tile(t)], wguT[:, 0, :], start=True, stop=True)\
                       .then_inc(gate1_psum, 1)

                def up1(t):
                    pe.wait_ge(sgf_done, count(prv, BEHIND["sgf_done"], 2 * t + 2))
                    mm(ps[:, 7, 0:INNER], xqT[:, tile(t)], wguT[:, 1, :], start=True, stop=True).then_inc(up1_psum, 1)

                def transpose_hq(t):
                    pe.wait_ge(hq_ready, count(prv, BEHIND["hq_ready"], t + 1))
                    for k in range(3):
                        ins = tr(ps[:, 7, tile(k)], hq[:, t % 2, tile(k)], idn)
                    ins.then_inc(hqT_psum, 1)

                def down1():
                    pe.wait_ge(hqT_ready, count(prv, BEHIND["hqT_ready"], 4))
                    for t in range(NT):
                        for k in range(3):
                            ins = mm(ps[:, 7, tile(t)], hqT[:, t, tile(k)], wdT[:, k, :],
                                     start=(k == 0), stop=(k == 2))
                    ins.then_inc(dn_psum, 1)

                steps = dict(
                    transpose0=transpose0, transpose1=transpose1, project_q=lambda: project(0),
                    project_k=lambda: project(1), project_v=project_v, row_max=row_max, shift_rows=shift_rows,
                    exps=exps, attend=attend, divide=divide, join=join, project_y=project_y,
                    transpose3=transpose3, route=route, transpose2=transpose2, keys1=keys1, queries1=queries1,
                    values1=values1, scores1=scores1, probs_T1=probs_T1, mix1=mix1, project1=project1,
                    transpose_xq=transpose_xq, gate1=gate1, up1=up1, transpose_hq=transpose_hq, down1=down1)
                walk(steps, dense, i, nxt, prv)

            pipeline(pe, run)


NAMES = ['L0_attn_x', 'L0_attn_W_K', 'L0_attn_W_Q', 'L0_attn_W_V', 'L0_attn_W_O', 'L0_ffn_ln1_w', 'L0_ffn_ln1_b',
         'L0_ffn_ln2_w', 'L0_ffn_ln2_b', 'L0_ffn_conv_w', 'L0_ffn_attn_w', 'L0_ffn_proj_w', 'L0_ffn_router_w',
         'L0_ffn_expert_wv', 'L0_ffn_expert_proj', 'L1_attn_qkv_w', 'L1_attn_qkv_b', 'L1_attn_proj_w',
         'L1_attn_proj_b', 'L1_ffn_w_gate', 'L1_ffn_w_up', 'L1_ffn_w_down']


def kernel(**inputs):
    import numpy as _np
    import concourse.bacc as _bacc
    from concourse.bass_utils import run_bass_kernel_spmd as _run

    nc = _bacc.Bacc("TRN2", target_bir_lowering=False, num_devices=1)
    arrays, aps = {}, {}
    for name in NAMES:
        a = _np.ascontiguousarray(inputs[name])
        arrays[f"in_{name}"] = a
        aps[name] = nc.dram_tensor(f"in_{name}", a.shape, F32, kind="ExternalInput").ap()
    arrays["in_constants"] = shape_constants()
    consts = nc.dram_tensor("in_constants", (P, K_END), F32, kind="ExternalInput").ap()
    shape = arrays["in_L0_attn_x"].shape
    out = nc.dram_tensor("out_0", shape, F32, kind="ExternalOutput").ap()
    build_layers(nc, aps, aps["L0_attn_x"], consts, out)
    r = _run(nc, [arrays], core_ids=[0])
    return r.results[0]["out_0"]
```
